# Optimizing a Trainium2 kernel written in Bass

```python
import numpy as np
import jax
import jax.numpy as jnp

def _softmax(x, axis=-1):
    return jax.nn.softmax(x, axis=axis)

def _gelu(x):
    return jax.nn.gelu(x, approximate=True)

def _silu(x):
    return jax.nn.silu(x)

def _sigmoid(x):
    return jax.nn.sigmoid(x)

def _layernorm(x, axis=-1, eps=1e-05):
    m = jnp.mean(x, axis=axis, keepdims=True)
    v = jnp.var(x, axis=axis, keepdims=True)
    return (x - m) / jnp.sqrt(v + eps)

def _scatter_add(tgt, idx, src, axis=0):
    return tgt.at[idx].add(src)

def _segment_sum(src, seg, n):
    return jax.ops.segment_sum(src, seg, n)
kernel_name = 'mk_recurrent_d2_jaxref_r8_f25901'

def setup_inputs(seed: int=0):
    np.random.seed(seed)
    _w = jnp.asarray

    def _L0_attn_setup():
        import jax, jax.numpy as jnp
        import numpy as np
        from jax import lax
        HID = 128
        NH = 16
        NKV = 4
        HD = 64
        SPLIT = 64
        KS = 3

        def _dynamic_conv(x, w_kgen, b_kgen, w_conv, b_conv):
            context = x.mean(axis=1)
            dyn = context @ w_kgen.T + b_kgen
            gate = jax.nn.sigmoid(dyn).mean(axis=1)
            x_t = x.transpose(0, 2, 1)
            y = lax.conv_general_dilated(x_t, w_conv, window_strides=(1,), padding=[(KS // 2, KS // 2)], feature_group_count=HID, dimension_numbers=('NCH', 'OIH', 'NCH'))
            y = (y + b_conv[None, :, None]) * gate[:, None, None]
            return y.transpose(0, 2, 1)

        def _fixed_split_attention(x, w_q, w_k, w_v, w_o):
            B, S, _ = x.shape
            q = (x @ w_q.T).reshape(B, S, NH, HD).transpose(0, 2, 1, 3)
            k = (x @ w_k.T).reshape(B, S, NKV, HD).transpose(0, 2, 1, 3)
            v = (x @ w_v.T).reshape(B, S, NKV, HD).transpose(0, 2, 1, 3)
            n_rep = NH // NKV
            k = jnp.repeat(k, n_rep, axis=1)
            v = jnp.repeat(v, n_rep, axis=1)
            C = S // SPLIT
            kc = k.reshape(B, NH, C, SPLIT, HD)
            vc = v.reshape(B, NH, C, SPLIT, HD)
            scale = HD ** (-0.5)
            scores = jnp.einsum('bhqd,bhckd->bhcqk', q, kc) * scale
            w = jax.nn.softmax(scores.astype(jnp.float32), axis=-1).astype(q.dtype)
            chunk_out = jnp.einsum('bhcqk,bhckd->bhcqd', w, vc)
            sum_w = w.sum(axis=-1, keepdims=True)
            combined = (chunk_out * sum_w).sum(axis=2)
            total = sum_w.sum(axis=2)
            out = combined / (total + 1e-09)
            out = out.transpose(0, 2, 1, 3).reshape(B, S, NH * HD)
            return out @ w_o.T
        key = jax.random.key(seed)
        ks = jax.random.split(key, 9)
        s = 0.02
        return {'hidden_states': jax.random.normal(ks[0], (2, 256, HID), jnp.float32), 'w_q': jax.random.normal(ks[1], (NH * HD, HID), jnp.float32) * s, 'w_k': jax.random.normal(ks[2], (NKV * HD, HID), jnp.float32) * s, 'w_v': jax.random.normal(ks[3], (NKV * HD, HID), jnp.float32) * s, 'w_o': jax.random.normal(ks[4], (HID, NH * HD), jnp.float32) * s, 'w_kgen': jax.random.normal(ks[5], (KS, HID), jnp.float32) * s, 'b_kgen': jnp.zeros((KS,), jnp.float32), 'w_conv': jax.random.normal(ks[6], (HID, 1, KS), jnp.float32) * s, 'b_conv': jnp.zeros((HID,), jnp.float32)}
    _L0_attn_in = _L0_attn_setup()

    def _L0_ffn_setup():
        import jax, jax.numpy as jnp
        import numpy as np
        D_MODEL = 128
        D_FF = 512
        NUM_EXPERTS = 8
        B, N = (16, 128)
        key = jax.random.key(seed)
        ks = jax.random.split(key, 7)
        s_in = 1.0 / np.sqrt(D_MODEL)
        s_ff = 1.0 / np.sqrt(D_FF)
        return {'x': jax.random.normal(ks[0], (B, N, D_MODEL), dtype=jnp.float32), 'Wr': jax.random.uniform(ks[1], (D_MODEL, NUM_EXPERTS), jnp.float32, -s_in, s_in), 'br': jax.random.uniform(ks[2], (NUM_EXPERTS,), jnp.float32, -s_in, s_in), 'W1': jax.random.uniform(ks[3], (NUM_EXPERTS, D_MODEL, D_FF), jnp.float32, -s_in, s_in), 'b1': jax.random.uniform(ks[4], (NUM_EXPERTS, D_FF), jnp.float32, -s_in, s_in), 'W2': jax.random.uniform(ks[5], (NUM_EXPERTS, D_FF, D_MODEL), jnp.float32, -s_ff, s_ff), 'b2': jax.random.uniform(ks[6], (NUM_EXPERTS, D_MODEL), jnp.float32, -s_ff, s_ff)}
    _L0_ffn_in = _L0_ffn_setup()

    def _L1_attn_setup():
        import jax, jax.numpy as jnp
        import numpy as np
        H = 8
        D = 64
        E = 128

        def sinusoidal_pe(T, d, dtype=jnp.float32):
            pos = jnp.arange(T, dtype=jnp.float32)[:, None]
            div = jnp.exp(jnp.arange(0, d, 2, dtype=jnp.float32) * (-np.log(10000.0) / d))
            ang = pos * div
            pe = jnp.stack([jnp.sin(ang), jnp.cos(ang)], axis=-1).reshape(T, d)
            return pe.astype(dtype)
        key = jax.random.key(seed)
        k1, k2, k3 = jax.random.split(key, 3)
        B, T = (2, 256)
        x = jax.random.normal(k1, (B, T, E), dtype=jnp.float32)
        Wqkv = jax.random.normal(k2, (3 * H * D, E), dtype=jnp.float32) * (1.0 / np.sqrt(E))
        Wo = jax.random.normal(k3, (E, H * D), dtype=jnp.float32) * (1.0 / np.sqrt(H * D))
        return {'x': x, 'Wqkv': Wqkv, 'Wo': Wo}
    _L1_attn_in = _L1_attn_setup()

    def _L1_ffn_setup():
        import jax, jax.numpy as jnp
        import numpy as np
        E = 16
        K = 4
        B, S, H, I = (4, 128, 128, 256)
        key = jax.random.key(seed)
        k0, k1, k2, k3 = jax.random.split(key, 4)
        scale = 0.02
        return {'hidden_states': jax.random.normal(k0, (B, S, H), jnp.float32), 'router_w': jax.random.normal(k1, (H, E), jnp.float32) * scale, 'router_b': jnp.zeros((E,), jnp.float32), 'w1': jax.random.normal(k2, (E, H, I), jnp.float32) * scale, 'b1': jnp.zeros((E, I), jnp.float32), 'w2': jax.random.normal(k3, (E, I, H), jnp.float32) * scale, 'b2': jnp.zeros((E, H), jnp.float32)}
    _L1_ffn_in = _L1_ffn_setup()
    _d = {'L0_attn_hidden_states': _L0_attn_in['hidden_states'], 'L0_attn_w_q': _L0_attn_in['w_q'], 'L0_attn_w_k': _L0_attn_in['w_k'], 'L0_attn_w_v': _L0_attn_in['w_v'], 'L0_attn_w_o': _L0_attn_in['w_o'], 'L0_attn_w_kgen': _L0_attn_in['w_kgen'], 'L0_attn_b_kgen': _L0_attn_in['b_kgen'], 'L0_attn_w_conv': _L0_attn_in['w_conv'], 'L0_attn_b_conv': _L0_attn_in['b_conv'], 'L0_ffn_Wr': _L0_ffn_in['Wr'], 'L0_ffn_br': _L0_ffn_in['br'], 'L0_ffn_W1': _L0_ffn_in['W1'], 'L0_ffn_b1': _L0_ffn_in['b1'], 'L0_ffn_W2': _L0_ffn_in['W2'], 'L0_ffn_b2': _L0_ffn_in['b2'], 'L1_attn_Wqkv': _L1_attn_in['Wqkv'], 'L1_attn_Wo': _L1_attn_in['Wo'], 'L1_ffn_router_w': _L1_ffn_in['router_w'], 'L1_ffn_router_b': _L1_ffn_in['router_b'], 'L1_ffn_w1': _L1_ffn_in['w1'], 'L1_ffn_b1': _L1_ffn_in['b1'], 'L1_ffn_w2': _L1_ffn_in['w2'], 'L1_ffn_b2': _L1_ffn_in['b2']}
    _x0 = _d['L0_attn_hidden_states']
    _d['L0_attn_hidden_states'] = jax.random.normal(jax.random.fold_in(jax.random.key(seed), 1), (4, 1024, 128), dtype=_x0.dtype)
    del _x0
    return _d

def reference(L0_attn_hidden_states, L0_attn_w_q, L0_attn_w_k, L0_attn_w_v, L0_attn_w_o, L0_attn_w_kgen, L0_attn_b_kgen, L0_attn_w_conv, L0_attn_b_conv, L0_ffn_Wr, L0_ffn_br, L0_ffn_W1, L0_ffn_b1, L0_ffn_W2, L0_ffn_b2, L1_attn_Wqkv, L1_attn_Wo, L1_ffn_router_w, L1_ffn_router_b, L1_ffn_w1, L1_ffn_b1, L1_ffn_w2, L1_ffn_b2):

    def _L0_attn_ref(hidden_states, w_q, w_k, w_v, w_o, w_kgen, b_kgen, w_conv, b_conv):
        import jax, jax.numpy as jnp
        import numpy as np
        from jax import lax
        HID = 128
        NH = 16
        NKV = 4
        HD = 64
        SPLIT = 64
        KS = 3

        def _dynamic_conv(x, w_kgen, b_kgen, w_conv, b_conv):
            context = x.mean(axis=1)
            dyn = context @ w_kgen.T + b_kgen
            gate = jax.nn.sigmoid(dyn).mean(axis=1)
            x_t = x.transpose(0, 2, 1)
            y = lax.conv_general_dilated(x_t, w_conv, window_strides=(1,), padding=[(KS // 2, KS // 2)], feature_group_count=HID, dimension_numbers=('NCH', 'OIH', 'NCH'))
            y = (y + b_conv[None, :, None]) * gate[:, None, None]
            return y.transpose(0, 2, 1)

        def _fixed_split_attention(x, w_q, w_k, w_v, w_o):
            B, S, _ = x.shape
            q = (x @ w_q.T).reshape(B, S, NH, HD).transpose(0, 2, 1, 3)
            k = (x @ w_k.T).reshape(B, S, NKV, HD).transpose(0, 2, 1, 3)
            v = (x @ w_v.T).reshape(B, S, NKV, HD).transpose(0, 2, 1, 3)
            n_rep = NH // NKV
            k = jnp.repeat(k, n_rep, axis=1)
            v = jnp.repeat(v, n_rep, axis=1)
            C = S // SPLIT
            kc = k.reshape(B, NH, C, SPLIT, HD)
            vc = v.reshape(B, NH, C, SPLIT, HD)
            scale = HD ** (-0.5)
            scores = jnp.einsum('bhqd,bhckd->bhcqk', q, kc) * scale
            w = jax.nn.softmax(scores.astype(jnp.float32), axis=-1).astype(q.dtype)
            chunk_out = jnp.einsum('bhcqk,bhckd->bhcqd', w, vc)
            sum_w = w.sum(axis=-1, keepdims=True)
            combined = (chunk_out * sum_w).sum(axis=2)
            total = sum_w.sum(axis=2)
            out = combined / (total + 1e-09)
            out = out.transpose(0, 2, 1, 3).reshape(B, S, NH * HD)
            return out @ w_o.T
        h = _dynamic_conv(hidden_states, w_kgen, b_kgen, w_conv, b_conv)
        return _fixed_split_attention(h, w_q, w_k, w_v, w_o)

    def _L0_ffn_ref(x, Wr, br, W1, b1, W2, b2):
        import jax, jax.numpy as jnp
        import numpy as np
        D_MODEL = 128
        D_FF = 512
        NUM_EXPERTS = 8
        B, N = (16, 128)
        scores = jnp.einsum('bh,he->be', x.mean(axis=1), Wr) + br
        top1 = jnp.argmax(scores, axis=-1)
        w1 = W1[top1]
        c1 = b1[top1]
        w2 = W2[top1]
        c2 = b2[top1]
        h = jax.nn.relu(jnp.einsum('bnh,bhf->bnf', x, w1) + c1[:, None, :])
        out = jnp.einsum('bnf,bfh->bnh', h, w2) + c2[:, None, :]
        return out

    def _L1_attn_ref(x, Wqkv, Wo):
        import jax, jax.numpy as jnp
        import numpy as np
        H = 8
        D = 64
        E = 128

        def sinusoidal_pe(T, d, dtype=jnp.float32):
            pos = jnp.arange(T, dtype=jnp.float32)[:, None]
            div = jnp.exp(jnp.arange(0, d, 2, dtype=jnp.float32) * (-np.log(10000.0) / d))
            ang = pos * div
            pe = jnp.stack([jnp.sin(ang), jnp.cos(ang)], axis=-1).reshape(T, d)
            return pe.astype(dtype)
        B, T, _ = x.shape
        qkv = jnp.einsum('bte,fe->btf', x, Wqkv)
        qkv = qkv.reshape(B, T, H, 3 * D)
        q, k, v = jnp.split(qkv, 3, axis=-1)
        q = q.transpose(0, 2, 1, 3)
        k = k.transpose(0, 2, 1, 3)
        v = v.transpose(0, 2, 1, 3)
        pe = sinusoidal_pe(T, D, q.dtype)
        q = q + pe[None, None]
        k = k + pe[None, None]
        causal = jnp.tril(jnp.ones((T, T), dtype=bool))
        scores = jnp.einsum('bhtd,bhsd->bhts', q, k) / jnp.sqrt(jnp.asarray(D, q.dtype))
        scores = jnp.where(causal[None, None], scores, jnp.asarray(-jnp.inf, q.dtype))
        probs = jax.nn.softmax(scores, axis=-1)
        attn = jnp.einsum('bhts,bhsd->bhtd', probs, v)
        out = attn.transpose(0, 2, 1, 3).reshape(B, T, H * D)
        out = jnp.einsum('btf,ef->bte', out, Wo)
        return out

    def _L1_ffn_ref(hidden_states, router_w, router_b, w1, b1, w2, b2):
        import jax, jax.numpy as jnp
        import numpy as np
        E = 16
        K = 4
        B, S, H, I = (4, 128, 128, 256)
        b, s, h = hidden_states.shape
        logits = hidden_states @ router_w + router_b
        probs = jax.nn.softmax(logits, axis=-1)
        topw, topi = jax.lax.top_k(probs, K)
        topw = topw / jnp.sum(topw, axis=-1, keepdims=True)
        combine = jnp.sum(jax.nn.one_hot(topi, E, dtype=hidden_states.dtype) * topw[..., None], axis=2)
        x = hidden_states.reshape(b * s, h)
        c = combine.reshape(b * s, E)

        def body(acc, expert):
            w1e, b1e, w2e, b2e, ce = expert
            hmid = jax.nn.gelu(x @ w1e + b1e, approximate=False)
            return (acc + (hmid @ w2e + b2e) * ce[:, None], None)
        out, _ = jax.lax.scan(body, jnp.zeros_like(x), (w1, b1, w2, b2, c.T))
        return out.reshape(b, s, h)
    x = L0_attn_hidden_states
    xn = _layernorm(x, axis=-1)
    s = _L0_attn_ref(xn, L0_attn_w_q, L0_attn_w_k, L0_attn_w_v, L0_attn_w_o, L0_attn_w_kgen, L0_attn_b_kgen, L0_attn_w_conv, L0_attn_b_conv)
    g = _silu(_L0_ffn_ref(xn, L0_ffn_Wr, L0_ffn_br, L0_ffn_W1, L0_ffn_b1, L0_ffn_W2, L0_ffn_b2))
    x = x + s * g
    xn = _layernorm(x, axis=-1)
    s = _L1_attn_ref(xn, L1_attn_Wqkv, L1_attn_Wo)
    g = _silu(_L1_ffn_ref(xn, L1_ffn_router_w, L1_ffn_router_b, L1_ffn_w1, L1_ffn_b1, L1_ffn_w2, L1_ffn_b2))
    x = x + s * g
    return x

_drawn_inputs = setup_inputs


def setup_inputs(seed=0):
    import zlib

    import numpy as np

    out = dict(_drawn_inputs(seed))
    spreads = {'L0_attn_b_kgen': (0.0, 0.8),
     'L0_attn_b_conv': (0.0, 0.8),
     'L1_ffn_router_b': (0.0, 0.8),
     'L1_ffn_b1': (0.0, 0.8),
     'L1_ffn_b2': (0.0, 0.8)}
    factors = {'L0_attn_w_q': 8.0,
     'L0_attn_w_k': 8.0,
     'L0_attn_w_v': 8.0,
     'L0_attn_w_o': 8.0,
     'L0_attn_w_kgen': 41.702,
     'L0_attn_w_conv': 8.0,
     'L0_ffn_Wr': 8.0,
     'L0_ffn_br': 8.0,
     'L0_ffn_W1': 8.0,
     'L0_ffn_b1': 8.0,
     'L0_ffn_W2': 8.0,
     'L0_ffn_b2': 8.0,
     'L1_attn_Wqkv': 8.0,
     'L1_attn_Wo': 8.0,
     'L1_ffn_router_w': 8.0,
     'L1_ffn_w1': 8.0,
     'L1_ffn_w2': 8.0}
    for name, (base, spread) in spreads.items():
        noise = np.random.default_rng([zlib.crc32(name.encode()), seed]).standard_normal(out[name].shape)
        drawn = base * np.exp(spread * noise) if base else spread * noise
        out[name] = jnp.asarray(drawn.astype(out[name].dtype))
    for name, factor in factors.items():
        out[name] = (out[name] * factor).astype(out[name].dtype)
    return out
```

```python
from contextlib import ExitStack

import numpy as np

import concourse.bass as bass
from concourse import mybir

F32, BF16, F16, U32 = (mybir.dt.float32, mybir.dt.bfloat16, mybir.dt.float16, mybir.dt.uint32)
ALU = mybir.AluOpType
ACT = mybir.ActivationFunctionType
AX = mybir.AxisListType.X
P = 128
BANK = 512
START = 1
EPS = 1e-5


def gated_layers(nc, x_in, w_q, w_k, w_v, w_o, w_kgen, b_kgen, w_conv, b_conv,
                 wr0, br0, w1_0, b1_0, w2_0, b2_0, w_qkv, w_o1, wr1, br1, w1_1, b1_1, w2_1, b2_1,
                 pos_t, out):
    B, S, C = x_in.shape
    D = 64
    NH = w_q.shape[0] // D
    NKV = w_k.shape[0] // D
    REP = NH // NKV
    T = S // P
    NT = B * T
    HALF = T // 2
    NCH = S // D
    OC = 2 * (D + 1)
    NS = 18
    E0, F0 = wr0.shape[1], w1_0.shape[2]
    E1, F1 = wr1.shape[1], w1_1.shape[2]
    NH1 = w_o1.shape[1] // D
    SCALE = float(D) ** -0.5
    MASKED = -1e30
    F16_MAX = 65504.0

    names = [("q", w_q), ("k", w_k), ("v", w_v), ("o", w_o), ("qkv", w_qkv), ("o1", w_o1)]
    col, n = {}, 0
    for name, w in names:
        col[name] = n
        n += w.shape[0] * w.shape[1] // C
    WCOLS = n

    ctx = ExitStack()
    with ctx:
        def sb(name, shape, dt=F32):
            return ctx.enter_context(nc.sbuf_tensor(name, shape, dt))

        def sem(name):
            return ctx.enter_context(nc.semaphore(name))

        ps = ctx.enter_context(nc.psum_tensor("ps", [P, 8, BANK], F32))
        x_sb = sb("x_sb", [P, NT, C])
        xnt = sb("xnt", [P, B, S + 2])
        big1 = sb("big1", [P, 2, 8, BANK])
        big2 = sb("big2", [P, T, NH * D])
        wt = sb("wt", [P, WCOLS])
        hcur = sb("hcur", [P, S])
        g_cur = sb("g_cur", [P, T, C])
        kst = sb("kst", [P, NKV, S], F16)
        kst2 = sb("kst2", [P, NKV, S], F16)
        vbd = sb("vbd", [P, NKV, T, OC])
        qhi = [sb(f"qhi{i}", [P, S], F16) for i in range(2)]
        q2 = [sb(f"q2{i}", [P, S], F16) for i in range(2)]
        wq_dup = [sb(f"wq_dup{i}", [P, P]) for i in range(2)]
        wk_dup = sb("wk_dup", [P, NKV, P])
        weighted_sb = [sb(f"weighted{i}", [P, NCH, D]) for i in range(2)]
        ident = sb("ident", [P, P])
        ident_h = sb("ident_h", [P, P], BF16)
        row_chunk = sb("row_chunk", [P, 16])
        ident_f16 = sb("ident_f16", [P, P], F16)
        negm = sb("negm", [P, HALF, 16])
        mhl = sb("mhl", [P, HALF, 32], F16)
        zinv = sb("zinv", [P, NS])
        coef = sb("coef", [P, NS])
        sumw = [sb(f"sumw{i}", [P, T, NS]) for i in range(2)]
        total = sb("total", [P, NH, T])
        tinv = sb("tinv", [P, NH, T])
        att_t = [sb(f"att_t{i}", [P, 8, P]) for i in range(2)]
        prod = [sb(f"prod{i}", [P, C]) for i in range(2)]
        stat = sb("stat", [P, 4, NT])
        ctx_mean = sb("ctx_mean", [P, B])
        kgen_t = sb("kgen_t", [P, 3])
        bkgen = sb("bkgen", [3, 1])
        sig = sb("sig", [3, B])
        third = sb("third", [3, P])
        gate = sb("gate", [P, B])
        conv_w = sb("conv_w", [P, 3])
        conv_b = sb("conv_b", [P, 1])
        conv_wg = sb("conv_wg", [P, B, 4])
        wr0_sb = sb("wr0_sb", [P, E0])
        br0_sb = sb("br0_sb", [1, E0])
        route = sb("route", [1, B, E0])
        route_max = sb("route_max", [1, B, 8])
        route_idx = sb("route_idx", [1, B, 8], U32)
        w1e = sb("w1e", [P, F0])
        w2e = sb("w2e", [P, F0 // P, C])
        b1e = sb("b1e", [P, F0 // P])
        b2e = sb("b2e", [1, C])
        ones_row = sb("ones_row", [1, P])
        vcur = sb("vcur", [P, T, OC])
        pos2 = vcur[:].rearrange("p t c -> p (t c)")[:, 0:S]
        mask_qk = sb("mask_qk", [P, P], BF16)
        mask_kq = sb("mask_kq", [P, P], BF16)
        negm1 = sb("negm1", [P, HALF, 1])
        zinv1 = sb("zinv1", [P, T])
        wr1_sb = sb("wr1_sb", [P, E1])
        br1_sb = sb("br1_sb", [P, E1])
        b1_sb = sb("b1_sb", [P, F1 // P, E1])
        b2_sb = sb("b2_sb", [E1, C])
        share = sb("share", [P, NT, E1])
        carry = sb("carry", [P, NT, E1])
        top8 = sb("top8", [P, NT, 8])
        acc = sb("acc", [P, 4, C])


        def named(*names):
            return [sem(name) for name in names]

        x_loaded = [sem(f"x_loaded{b}") for b in range(B)]
        weights_loaded, small_loaded, expert_loaded, stored = named(
            "weights_loaded", "small_loaded", "expert_loaded", "stored")
        ident_ready, pool_step, consts_ready, spread_ready, zeros_ready = named(
            "ident_ready", "pool_step", "consts_ready", "spread_ready", "zeros_ready")
        w_psum, w_copied = named("w_psum", "w_copied")
        dve_step, centered, squared, var_ready, std_ready, normed, xt_psum, xt_copied = named(
            "dve_step", "centered", "squared", "var_ready", "std_ready", "normed", "xt_psum", "xt_copied")
        ctx_ready, dyn_psum, sig_ready, gate_psum, route_psum, route_ready = named(
            "ctx_ready", "dyn_psum", "sig_ready", "gate_psum", "route_psum", "route_ready")
        conv_ready, conv_step = named("conv_ready", "conv_step")
        f1_psum, f1_ready, f2_psum, g_ready = named("f1_psum", "f1_ready", "f2_psum", "g_ready")
        wk_ready, k_psum, k_hi, k_ready, v_psum, v_ready, vcur_ready, wq_ready, q_psum, q_hi, q_ready = named(
            "wk_ready", "k_psum", "k_hi", "k_ready", "v_psum", "v_ready", "vcur_ready", "wq_ready", "q_psum", "q_hi",
            "q_ready")
        s_psum, s_max, mhi_ready, m_ready, mt_psum, mt_ready = named(
            "s_psum", "s_max", "mhi_ready", "m_ready", "mt_psum", "mt_ready")
        st_psum, e_ready, pv_psum, inv_ready, sumw_ready, coef_ready, weighted_a, weighted_b, weighted = named(
            "st_psum", "e_ready", "pv_psum", "inv_ready", "sumw_ready", "coef_ready", "weighted_a",
            "weighted_b", "weighted")
        tree_step, chunks_summed, total_ready = named("tree_step", "chunks_summed", "total_ready")
        tinv_ready, att_normed, at_psum, at_ready, y_psum, prod_ready, x_ready = named(
            "tinv_ready", "att_normed", "at_psum", "at_ready", "y_psum", "prod_ready", "x_ready")

        logits_psum, shifted, r_exp, share_ready, st_psum1, e_ready1 = named(
            "logits_psum", "shifted", "r_exp", "share_ready", "st_psum1", "e_ready1")
        ct_psum, ct_ready, b2_psum, b2_ready, experts_loaded = named(
            "ct_psum", "ct_ready", "b2_psum", "b2_ready", "experts_loaded")
        up_psum, up_ready, down_psum, acc_ready, gate1_ready, pos_loaded, ones_ready, masks_ready = named(
            "up_psum", "up_ready", "down_psum", "acc_ready", "gate1_ready", "pos_loaded", "ones_ready",
            "masks_ready")
        h1_ready, v1_psum, v1_ready, w1_ready, qk_psum, qkf_ready, qk_hi, qk_ready = named(
            "h1_ready", "v1_psum", "v1_ready", "w1_ready", "qk_psum", "qkf_ready", "qk_hi", "qk_ready")
        s1_psum, s1_max, mhi1_ready, m1_ready, mt1_psum, mt1_ready, pv1_psum, inv1_ready, att1_ready = named(
            "s1_psum", "s1_max", "mhi1_ready", "m1_ready", "mt1_psum", "mt1_ready", "pv1_psum", "inv1_ready",
            "att1_ready")
        at1_psum, at1_ready, y1_psum, prod1_ready, x1_ready = named(
            "at1_psum", "at1_ready", "y1_psum", "prod1_ready", "x1_ready")

        flat1 = big1[:].rearrange("p a b c -> p (a b c)")
        flat2 = big2[:].rearrange("p a b -> p (a b)")
        up_w = flat1[:, 0:E1 * F1].rearrange("p (e f) -> p e f", e=E1)
        down_w = flat1[:, E1 * F1:2 * E1 * F1].rearrange("p (e f c) -> p e f c", e=E1, f=F1 // P)
        gate1 = flat2[:, 0:NT * C].rearrange("p (t c) -> p t c", c=C)
        att1 = flat2[:, NT * C:NT * C + T * NH1 * D].rearrange("p (t f) -> p t f", t=T)
        mid1 = flat2[:, NT * C:NT * C + 4 * 2 * BANK].rearrange("p (a f t) -> p a f t", a=4, f=F1 // P)
        rt = [flat2[:, NT * C + i * BANK:NT * C + (i + 1) * BANK].rearrange("p (t e) -> p t e", e=E1)
              for i in range(7)]
        qkf = [w[:].rearrange("p a b -> p (a b)") for w in weighted_sb]
        v1 = vbd[:].rearrange("p k t c -> p (k t c)").rearrange("p (h t c) -> p h t c", h=NH1, t=T)
        NU = HALF + T
        PARTS = [(0, 0), (1, 0), (0, 1), (1, 1)]
        NP = len(PARTS)
        NV = T // 2
        UNITS = [[(0, blk) for blk in range(HALF)], [(1, blk) for blk in range(T)]]

        xn = big1[:].rearrange("p a b c -> p (a b c)")[:, 0:NT * C].rearrange("p (t c) -> p t c", c=C)
        sq = big1[:].rearrange("p a b c -> p (a b c)")[:, NT * C:2 * NT * C].rearrange("p (t c) -> p t c", c=C)
        wraw = big2[:].rearrange("p a b -> p (a b)")[:, 0:WCOLS]
        hmid = big2[:].rearrange("p a b -> p (a b)")[:, 0:F0 // P * S].rearrange("p (f t) -> p f t", f=F0 // P)
        MROWS = slice(D, D + 32)
        mt_ps = ps[:, 7, :].bitcast(F16)[:, 0:P]
        o_ps = ps[:, 4:7, 0:3 * OC].rearrange("p a (b c) -> p a b c", c=D + 1)
        s_ps = ps[:, 0:2, :].rearrange("p a b -> p (a b)")
        W1B = S // BANK

        def wide(ap, n):
            shape = list(ap.shape) + [n]
            return ap.unsqueeze(len(ap.shape)).to_broadcast(shape)

        def product_place(blk):
            return (6, blk) if blk < 2 else (4 + (blk - 2) // 3, (blk - 2) % 3)

        def places(ap):
            return ap.rearrange("p (a b) -> p a b", a=3)

        def chain(signal, ins, eng, tally):
            tally[0] += 1
            ins.then_inc(signal, 1)
            eng.wait_ge(signal, tally[0])

        def each_head(eng, b, do):
            with eng.Fori(0, NKV - 1) as g:
                for j in range(REP):
                    do(b * NH + g * REP + j, g, j, 3)
            for j in range(REP):
                do(b * NH + (NKV - 1) * REP + j, NKV - 1, j, REP - 1 - j)

        def each_sequence(eng, do):
            with eng.Fori(0, B - 1) as b:
                do(b, True)
            do(B - 1, False)

        def each_head1(eng, b, do):
            with eng.Fori(0, NH1 // 2 - 1) as g:
                for p in range(2):
                    do(b * NH1 + g * 2 + p, g * 2 + p, p, 3)
            for p in range(2):
                do(b * NH1 + NH1 - 2 + p, NH1 - 2 + p, p, 1 - p)

        def unit_index(half, blk):
            return half * HALF + blk

        def unit_cols(half, blk):
            return max(0, blk - half * HALF) * P

        block = ctx.enter_context(nc.Block())

        @block.sync
        def _(sp):
            for b in range(B):
                sp.dma_start(x_sb[:, b * T:(b + 1) * T, :],
                             x_in[b].rearrange("(t p) c -> p t c", p=P)).then_inc(x_loaded[b], 16)
            for name, w in names:
                dst = wraw[:, col[name]:col[name] + w.shape[0] * w.shape[1] // C]
                if w.shape[1] == C:
                    sp.dma_start(dst.rearrange("p (n c) -> p n c", c=C),
                                 w.rearrange("(n p) c -> p n c", p=P)).then_inc(weights_loaded, 16)
                else:
                    sp.dma_start(dst, w).then_inc(weights_loaded, 16)
            sp.dma_start(kgen_t[:], w_kgen.rearrange("k c -> c k"),
                         allow_slow_non_contiguous=True).then_inc(small_loaded, 16)
            sp.dma_start(bkgen[:], b_kgen.rearrange("(k a) -> k a", a=1)).then_inc(small_loaded, 16)
            sp.dma_start(conv_w[:], w_conv.rearrange("c a k -> c (a k)")).then_inc(small_loaded, 16)
            sp.dma_start(conv_b[:], b_conv.rearrange("(c a) -> c a", a=1)).then_inc(small_loaded, 16)
            sp.dma_start(wr0_sb[:], wr0).then_inc(small_loaded, 16)
            sp.dma_start(br0_sb[:], br0.rearrange("(a e) -> a e", a=1)).then_inc(small_loaded, 16)
            sp.dma_start(wr1_sb[:], wr1).then_inc(pos_loaded, 16)
            sp.dma_start(br1_sb[:], br1.rearrange("(a e) -> a e", a=1).to_broadcast([P, E1])).then_inc(pos_loaded, 16)
            sp.dma_start(b2_sb[:], b2_1).then_inc(pos_loaded, 16)
            for f in range(F1 // P):
                sp.dma_start(b1_sb[:, f, :], b1_1[:, f * P:(f + 1) * P].rearrange("e p -> p e"),
                             allow_slow_non_contiguous=True).then_inc(pos_loaded, 16)
            sp.wait_ge(route_ready, 1)
            with sp.Fori(0, B) as b:
                sp.wait_ge(g_ready, START + b * T)
                e = sp.value_load(route_idx[0:1, b, 0:1], min_val=0, max_val=E0 - 1)
                sp.dma_start(w1e[:], w1_0[e]).then_inc(expert_loaded, 16)
                sp.dma_start(w2e[:], w2_0[e].rearrange("(n p) c -> p n c", p=P)).then_inc(expert_loaded, 16)
                sp.dma_start(b1e[:], b1_0[e].rearrange("(n p) -> p n", p=P),
                             allow_slow_non_contiguous=True).then_inc(expert_loaded, 16)
                sp.dma_start(b2e[:], b2_0[e].rearrange("(a c) -> a c", a=1)).then_inc(expert_loaded, 16)
            sp.wait_ge(x_ready, B * T)
            sp.dma_start(pos2[0:D, :], pos_t).then_inc(pos_loaded, 16)
            sp.dma_start(pos2[D:P, :], pos_t).then_inc(pos_loaded, 16)
            sp.wait_ge(xt_psum, 2 * B * W1B)
            sp.dma_start(up_w, w1_1.rearrange("e c f -> c e f")).then_inc(experts_loaded, 16)
            for f in range(F1 // P):
                sp.dma_start(down_w[:, :, f, :], w2_1[:, f * P:(f + 1) * P, :].rearrange("e p c -> p e c")).then_inc(experts_loaded, 16)
            for b in range(B):
                sp.wait_ge(x1_ready, (b + 1) * T)
                sp.dma_start(out[b].rearrange("(t p) c -> p t c", p=P),
                             x_sb[:, b * T:(b + 1) * T, :]).then_inc(stored, 16)
            sp.wait_ge(stored, 16 * B)

        @block.gpsimd
        def _(pool):
            step = [0]
            chain(pool_step, nc.gpsimd.memset(ident[:], 0.0), pool, step)
            nc.gpsimd.affine_select(out=ident[:], in_=ident[:], compare_op=ALU.not_equal, fill=1.0, base=0,
                                    pattern=[[-1, P]], channel_multiplier=1).then_inc(ident_ready, 1)
            nc.gpsimd.memset(xnt[:, :, 0:1], 0.0)
            nc.gpsimd.memset(xnt[:, :, S + 1:S + 2], 0.0)
            nc.gpsimd.memset(third[:], 1.0 / 3.0)
            nc.gpsimd.memset(ones_row[:], 1.0).then_inc(consts_ready, 1)
            chain(pool_step, nc.gpsimd.memset(vbd[:], 0.0), pool, step)
            nc.gpsimd.memset(vbd[0:D, :, :, D:D + 1], 1.0)
            chain(pool_step, nc.gpsimd.memset(vbd[D:P, :, :, OC - 1:OC], 1.0), pool, step)
            nc.gpsimd.memset(kst2[:], 0.0)
            nc.gpsimd.memset(q2[0][:], 0.0)
            nc.gpsimd.memset(q2[1][:], 0.0).then_inc(zeros_ready, 1)
            chain(pool_step, nc.gpsimd.memset(mask_qk[:], 0.0), pool, step)
            chain(pool_step, nc.gpsimd.memset(mask_kq[:], 0.0), pool, step)
            nc.gpsimd.affine_select(out=mask_qk[:], in_=mask_qk[:], compare_op=ALU.is_ge, fill=MASKED, base=0,
                                    pattern=[[-1, P]], channel_multiplier=1)
            nc.gpsimd.affine_select(out=mask_kq[:], in_=mask_kq[:], compare_op=ALU.is_ge, fill=MASKED, base=0,
                                    pattern=[[1, P]], channel_multiplier=-1)
            chain(pool_step, nc.gpsimd.memset(carry[:], 1.0), pool, step)
            nc.gpsimd.memset(carry[:, :, 0:1], 0.0).then_inc(masks_ready, 1)
            pool.nop().then_inc(chunks_summed, 2)
            pool.wait_ge(w_copied, WCOLS // BANK)
            for kv in range(NKV):
                wk = wt[:, col["k"] + kv * D:col["k"] + (kv + 1) * D]
                nc.gpsimd.tensor_copy(wk_dup[:, kv, 0:D], wk)
                last = nc.gpsimd.tensor_copy(wk_dup[:, kv, D:P], wk)
            last.then_inc(wk_ready, 1)

            def stage_wq(H, g, j, p):
                pool.nop(nofuse=True)
                src = wt[:, bass.ds(col["q"] + g * REP * D + j * D, D)]
                nc.gpsimd.tensor_copy(wq_dup[p][:, 0:D], src)
                nc.gpsimd.tensor_copy(wq_dup[p][:, D:P], src).then_inc(wq_ready, 1)

            def sequence(b, more):
                pool.wait_ge(q_psum, START + b * NH)
                stage_wq(b * NH, 0, 0, 0)
                stage_wq(b * NH + 1, 0, 1, 1)

                def head(H, g, j, left):
                    if left >= 2:
                        pool.wait_ge(q_psum, START + H + 1)
                        stage_wq(H + 2, g, j + 2, j % 2)
                    for t in range(T):
                        n = H * T + t
                        w = weighted_sb[t % 2]
                        pool.wait_ge(weighted, START + n + 1)
                        nc.gpsimd.tensor_tensor(w[:, 0:8, :], w[:, 0:8, :], w[:, 8:16, :], ALU.add).then_inc(tree_step, 1)
                        pool.wait_ge(tree_step, n * 3 + 1)
                        nc.gpsimd.tensor_tensor(w[:, 0:4, :], w[:, 0:4, :], w[:, 4:8, :], ALU.add).then_inc(tree_step, 1)
                        pool.wait_ge(tree_step, n * 3 + 2)
                        nc.gpsimd.tensor_tensor(w[:, 0:2, :], w[:, 0:2, :], w[:, 2:4, :], ALU.add).then_inc(tree_step, 1)
                        pool.wait_ge(tree_step, n * 3 + 3)
                        nc.gpsimd.tensor_tensor(big2[:, t, bass.ds(g * REP * D + j * D, D)], w[:, 0, :], w[:, 1, :],
                                                ALU.add).then_inc(chunks_summed, 1)

                each_head(pool, b, head)

            each_sequence(pool, sequence)

            pool.wait_ge(x_ready, B * T)
            chain(pool_step, nc.gpsimd.memset(kst2[MROWS, 0:2, :], 1.0), pool, step)
            nc.gpsimd.memset(v1[:, :, :, D:D + 1], 1.0).then_inc(ones_ready, 1)
            with pool.Fori(0, B) as b:
                def stage_qk(H, h, p):
                    pool.nop(nofuse=True)
                    for i, dst in enumerate((wq_dup[p][:], wk_dup[:, p, :])):
                        src = wt[:, bass.ds(col["qkv"] + h * 3 * D + i * D, D)]
                        nc.gpsimd.tensor_copy(dst[:, 0:D], src)
                        last = nc.gpsimd.tensor_copy(dst[:, D:P], src)
                    last.then_inc(w1_ready, 1)

                pool.wait_ge(qk_psum, START + b * NH1 * NP)
                stage_qk(b * NH1, 0, 0)
                stage_qk(b * NH1 + 1, 1, 1)

                def head1(H, h, p, left):
                    if left >= 2:
                        pool.wait_ge(qk_psum, START + (H + 1) * NP)
                        stage_qk(H + 2, h + 2, p)

                each_head1(pool, b, head1)

        @block.scalar
        def _(act):
            for started in (g_ready, mt_ready, mt1_ready):
                act.nop().then_inc(started, START)
            def norm_act(L):
                for b in range(B):
                    act.wait_ge(centered, L * B + b + 1)
                    nc.scalar.activation(sq[:, b * T:(b + 1) * T, :], xn[:, b * T:(b + 1) * T, :],
                                         ACT.Square).then_inc(squared, 1)
                for b in range(B):
                    act.wait_ge(var_ready, L * B + b + 1)
                    nc.scalar.activation(stat[:, 3, b * T:(b + 1) * T], stat[:, 2, b * T:(b + 1) * T],
                                         ACT.Sqrt).then_inc(std_ready, 1)
                for u in range(B * W1B):
                    act.wait_ge(xt_psum, L * B * W1B + u + 1)
                    nc.scalar.copy(xnt[:, u // W1B, bass.ds(1 + u % W1B * BANK, BANK)], ps[:, u % 2, :]).then_inc(xt_copied, 1)

            norm_act(0)
            for u in range(WCOLS // BANK):
                act.wait_ge(w_psum, u + 1)
                nc.scalar.copy(wt[:, u * BANK:(u + 1) * BANK], ps[:, 2 + u % 2, :]).then_inc(w_copied, 1)
            act.wait_ge(dyn_psum, 1)
            act.wait_ge(small_loaded, 16 * 6)
            nc.scalar.activation(sig[:], ps[0:3, 4, 0:B], ACT.Sigmoid, bias=bkgen[:, 0:1]).then_inc(sig_ready, 1)
            act.wait_ge(zeros_ready, 1)

            def copy_keys(b, kv):
                act.wait_ge(k_psum, b * NKV + kv + 1)
                k_ps = ps[:, 2 * (kv % 2):2 * (kv % 2) + 2, :].rearrange("p a b -> p (a b)")
                nc.scalar.copy(kst[:, kv, :], k_ps)
                nc.scalar.copy(kst2[0:D, kv, :], k_ps[0:D]).then_inc(k_hi, 1)

            def copy_values(b, i):
                act.wait_ge(v_psum, b * NV + i + 1)
                v_ps = ps[:, 7, :].rearrange("p (t k d) -> p t k d", t=2, d=D)
                for t in range(2):
                    nc.scalar.copy(vbd[0:D, :, 2 * i + t, 0:D], v_ps[0:D, t])
                    last = nc.scalar.copy(vbd[D:P, :, 2 * i + t, D + 1:OC - 1], v_ps[D:P, t])
                last.then_inc(v_ready, 1)

            for i in range(NKV):
                copy_keys(0, i)
                copy_values(0, i)

            def sequence(b, more):
                def q_leading(H, p):
                    act.wait_ge(q_psum, START + H + 1)
                    nc.scalar.mul(qhi[p][:], s_ps, SCALE).then_inc(q_hi, 1)

                def max_rows(H, p, half):
                    act.wait_ge(mt_psum, START + H * 2 + half + 1)
                    for t in range(HALF):
                        c0 = half * BANK + t * P
                        last = nc.scalar.copy(q2[p][MROWS, c0:c0 + P], mt_ps[32 * t:32 * t + 32, :])
                    last.then_inc(mt_ready, 1)

                def exps(H, half, units, tiles_done=None):
                    for blk in units:
                        u = H * 16 + half * 8 + blk
                        act.wait_ge(st_psum, u + 1)
                        if tiles_done is not None:
                            act.wait_ge(pv_psum, START + tiles_done)
                        nc.scalar.activation(big1[:, half, blk, :], ps[:, 2 + blk % 2, :],
                                             ACT.Exp).then_inc(e_ready, 1)

                def hidden(units):
                    for u in units:
                        f, half = u // W1B, u % W1B
                        act.wait_ge(f1_psum, b * 8 + u + 1)
                        nc.scalar.activation(hmid[:, f, half * BANK:(half + 1) * BANK], ps[:, 4 + u % 2, :], ACT.Relu,
                                             bias=b1e[:, f:f + 1]).then_inc(f1_ready, 1)

                def take_values(g):
                    for t in (0, HALF):
                        nc.scalar.copy(vcur[:, t:t + HALF, :], vbd[:, g, t:t + HALF, :]).then_inc(vcur_ready, 1)

                q_leading(b * NH, 0)
                act.wait_ge(expert_loaded, b * 64 + 64)
                hidden(range(4))
                q_leading(b * NH + 1, 1)
                hidden(range(4, 8))
                act.wait_ge(v_ready, (b + 1) * NV)
                take_values(0)
                act.wait_ge(prod_ready, START + b * T)
                for t in range(T):
                    act.wait_ge(f2_psum, b * T + t + 1)
                    nc.scalar.activation(g_cur[:, t, :], ps[:, 2 + t % 2, 0:C], ACT.Silu).then_inc(g_ready, 1)
                max_rows(b * NH, 0, 0)
                exps(b * NH, 0, range(8))

                def head(H, g, j, left):
                    p = j % 2
                    max_rows(H, p, 1)
                    for t in range(T):
                        if t < HALF:
                            exps(H, 1, (2 * t, 2 * t + 1), H * T)
                        elif left >= 1:
                            if t == HALF:
                                max_rows(H + 1, 1 - p, 0)
                            exps(H + 1, 0, (2 * t - 8, 2 * t - 7), H * T + HALF)
                        if t == HALF and left >= 2:
                            q_leading(H + 2, j % 2)
                        if t >= HALF and left == 0 and more:
                            copy_keys(b + 1, t - HALF)
                            copy_values(b + 1, t - HALF)
                    if j == REP - 1 and left >= 1:
                        act.wait_ge(pv_psum, START + H * T + T)
                        take_values(g + 1)

                each_head(act, b, head)
                for t in range(T):
                    act.wait_ge(at_psum, b * T + t + 1)
                    a_ps = ps[:, 2 * (t % 2):2 * (t % 2) + 2, :].rearrange("p a b -> p (a b)")
                    if t >= 2:
                        act.wait_ge(y_psum, b * T + t - 1)
                    nc.scalar.copy(att_t[t % 2][:].rearrange("p a b -> p (a b)"), a_ps).then_inc(at_ready, 1)

            each_sequence(act, sequence)

            norm_act(1)
            act.wait_ge(shifted, 1)
            nc.scalar.activation(rt[1], rt[0], ACT.Exp).then_inc(r_exp, 1)
            for u in range(NT // 4):
                act.wait_ge(ct_psum, u + 1)
                nc.scalar.copy(att_t[u % 2][0:E1, 0:4, :].rearrange("p a b -> p (a b)"), ps[0:E1, u % 2, :]).then_inc(ct_ready, 1)
                act.wait_ge(b2_psum, u + 1)
                nc.scalar.copy(gate1[:, 4 * u:4 * u + 4, :].rearrange("p a b -> p (a b)"), ps[:, 2 + u % 2, :]).then_inc(b2_ready, 1)
            with act.Fori(0, NT // 4) as k:
                for e in range(E1):
                    for f in range(F1 // P):
                        u = k * E1 * 2 + e * 2 + f
                        act.wait_ge(up_psum, u + 1)
                        nc.scalar.activation(mid1[:, e % 4, f, :], ps[:, 2 * (e % 2) + f, :], ACT.Gelu,
                                             bias=b1_sb[:, f, e:e + 1]).then_inc(up_ready, 1)
            act.wait_ge(acc_ready, START + NT // 4 * E1 * 4)
            nc.scalar.activation(gate1, gate1, ACT.Silu).then_inc(gate1_ready, 1)
            with act.Fori(0, B) as b:
                for t in range(T):
                    act.wait_ge(v1_psum, b * T + t + 1)
                    nc.scalar.copy(v1[:, :, t, 0:D], ps[:, 4 + t % 2, :].rearrange("p (h d) -> p h d", d=D)).then_inc(v1_ready, 1)

                def leading(H, p, i):
                    which, half = PARTS[i]
                    cols = slice(half * BANK, (half + 1) * BANK)
                    act.wait_ge(qkf_ready, START + H * NP + i + 1)
                    if which == 0:
                        nc.scalar.mul(qhi[p][:, cols], qkf[0][:, cols], SCALE).then_inc(qk_hi, 1)
                    else:
                        nc.scalar.copy(kst[:, p, cols], qkf[1][:, cols])
                        nc.scalar.copy(kst2[0:D, p, cols], qkf[1][0:D, cols]).then_inc(qk_hi, 1)

                def max_rows1(H, p, half):
                    act.wait_ge(mt1_psum, START + H * 2 + half + 1)
                    for t in range(HALF):
                        c0 = half * BANK + t * P
                        last = nc.scalar.copy(q2[p][MROWS, c0:c0 + P], mt_ps[32 * t:32 * t + 32, :])
                    last.then_inc(mt1_ready, 1)

                def exps1(H, units, tiles_done=None):
                    for half, blk in units:
                        u = H * NU + unit_index(half, blk)
                        act.wait_ge(st_psum1, u + 1)
                        if tiles_done is not None:
                            act.wait_ge(pv1_psum, START + tiles_done)
                        c0 = unit_cols(half, blk)
                        nc.scalar.activation(big1[:, half, blk, c0:BANK], ps[:, 2 + blk % 2, c0:BANK],
                                             ACT.Exp).then_inc(e_ready1, 1)

                for p in range(2):
                    for i in range(NP):
                        leading(b * NH1 + p, p, i)
                max_rows1(b * NH1, 0, 0)
                exps1(b * NH1, UNITS[0])

                def head1(H, h, p, left):
                    max_rows1(H, p, 1)
                    for t in range(T):
                        if t < HALF:
                            exps1(H, UNITS[1][2 * t:2 * t + 2], H * T)
                        elif left >= 1:
                            if t == HALF:
                                max_rows1(H + 1, 1 - p, 0)
                            exps1(H + 1, UNITS[0][t - HALF:t - HALF + 1], H * T + HALF)
                        if t >= HALF and left >= 2:
                            leading(H + 2, p, t - HALF)

                each_head1(act, b, head1)
                for t in range(T):
                    act.wait_ge(at1_psum, b * T + t + 1)
                    if t >= 2:
                        act.wait_ge(y1_psum, b * T + t - 1)
                    nc.scalar.copy(att_t[t % 2][:, 0:4, :].rearrange("p a b -> p (a b)"), ps[:, t % 2, :]).then_inc(at1_ready, 1)

        @block.vector
        def _(dve):
            step = [0]
            for started in (prod_ready, m_ready, weighted, weighted_a, weighted_b, acc_ready, m1_ready, att1_ready,
                            qkf_ready):
                dve.nop().then_inc(started, START)
            dve.nop().then_inc(qk_ready, NP)

            def do(ins):
                chain(dve_step, ins, dve, step)

            dve.wait_ge(ident_ready, 1)
            do(nc.vector.tensor_copy(ident_h[:], ident[:]))
            do(nc.vector.tensor_reduce(row_chunk[:], ident[:].rearrange("p (s c) -> p c s", c=16), AX, ALU.add))
            nc.vector.tensor_copy(ident_f16[:], ident[:])
            dve.wait_ge(zeros_ready, 1)
            for kv in range(NKV):
                last = nc.vector.tensor_copy(kst2[MROWS, kv, :].rearrange("p (c k) -> p c k", k=D),
                                             wide(row_chunk[MROWS, :], D))
            last.then_inc(spread_ready, 1)
            do(nc.vector.memset(ps[:, 6, 2 * OC:3 * OC], 0.0))
            do(nc.vector.memset(o_ps[:, 2, 4:6, D:D + 1], 1.0))

            def norm_dve(L):
                bs = lambda b: slice(b * T, (b + 1) * T)
                for b in range(B):
                    if L == 0:
                        dve.wait_ge(x_loaded[b], 16)
                    do(nc.vector.tensor_reduce(stat[:, 0, bs(b)], x_sb[:, bs(b), :], AX, ALU.add))
                    do(nc.vector.tensor_scalar(stat[:, 1, bs(b)], stat[:, 0, bs(b)], 1.0 / C, None, ALU.mult))
                    nc.vector.tensor_tensor(xn[:, bs(b), :], x_sb[:, bs(b), :], wide(stat[:, 1, bs(b)], C),
                                            ALU.subtract).then_inc(centered, 1)
                for b in range(B):
                    dve.wait_ge(squared, L * B + b + 1)
                    do(nc.vector.tensor_reduce(stat[:, 0, bs(b)], sq[:, bs(b), :], AX, ALU.add))
                    nc.vector.tensor_scalar(stat[:, 2, bs(b)], stat[:, 0, bs(b)], 1.0 / C, EPS, ALU.mult,
                                            ALU.add).then_inc(var_ready, 1)
                for b in range(B):
                    dve.wait_ge(std_ready, L * B + b + 1)
                    do(nc.vector.reciprocal(stat[:, 0, bs(b)], stat[:, 3, bs(b)]))
                    dve.wait_ge(centered, L * B + b + 1)
                    nc.vector.tensor_tensor(xn[:, bs(b), :], xn[:, bs(b), :], wide(stat[:, 0, bs(b)], C),
                                            ALU.mult).then_inc(normed, 1)

            norm_dve(0)
            for b in range(B):
                dve.wait_ge(xt_copied, W1B * (b + 1))
                do(nc.vector.tensor_reduce(stat[:, 1, b:b + 1], xnt[:, b, 1:S + 1], AX, ALU.add))
            nc.vector.tensor_scalar(ctx_mean[:], stat[:, 1, 0:B], 1.0 / S, None, ALU.mult).then_inc(ctx_ready, 1)
            dve.wait_ge(route_psum, 1)
            for b in range(B):
                do(nc.vector.tensor_tensor(route[:, b, :], ps[0:1, 5, b * E0:(b + 1) * E0], br0_sb[:], ALU.add))
                do(nc.vector.max(route_max[:, b, :], route[:, b, :]))
                last = nc.vector.max_index(route_idx[:, b, :], route_max[:, b, :], route[:, b, :])
                if b < B - 1:
                    do(last)
            last.then_inc(route_ready, 1)
            dve.wait_ge(gate_psum, 1)
            do(nc.vector.tensor_copy(gate[:], ps[:, 4, 8:8 + B]))
            for b in range(B):
                do(nc.vector.tensor_scalar(conv_wg[:, b, 0:3], conv_w[:], gate[:, b:b + 1], None, ALU.mult))
                do(nc.vector.tensor_tensor(conv_wg[:, b, 3:4], conv_b[:], gate[:, b:b + 1], ALU.mult))

            def convolve(b, k):
                wg = lambda k: conv_wg[:, b, k:k + 1]
                if k == 0:
                    nc.vector.tensor_scalar(hcur[:], xnt[:, b, 1:S + 1], wg(1), wg(3), ALU.mult,
                                            ALU.add).then_inc(conv_step, 1)
                else:
                    dve.wait_ge(conv_step, b * 2 + k)
                    first = 0 if k == 1 else 2
                    nc.vector.scalar_tensor_tensor(out=hcur[:], in0=xnt[:, b, first:first + S], scalar=wg(first),
                                                   in1=hcur[:], op0=ALU.mult,
                                                   op1=ALU.add).then_inc(conv_step if k == 1 else conv_ready, 1)

            def keys_rest(b, kv):
                dve.wait_ge(k_hi, b * NKV + kv + 1)
                k_ps = ps[:, 2 * (kv % 2):2 * (kv % 2) + 2, :].rearrange("p a b -> p (a b)")
                nc.vector.tensor_tensor(kst[D:P, kv, :], k_ps[D:P], kst[D:P, kv, :], ALU.subtract).then_inc(k_ready, 1)

            for k in range(3):
                convolve(0, k)
            for kv in range(NKV):
                keys_rest(0, kv)

            def sequence(b, more):
                def q_rest(H, p):
                    dve.wait_ge(q_hi, H + 1)
                    nc.vector.scalar_tensor_tensor(out=q2[p][0:D, :], in0=s_ps[0:D], scalar=SCALE, in1=qhi[p][0:D, :],
                                                   op0=ALU.mult, op1=ALU.subtract).then_inc(q_ready, 1)

                def maxima(H, t, bank=0):
                    dve.wait_ge(s_psum, H * T + t + 1)
                    if t % HALF == 0:
                        dve.wait_ge(m_ready, START + H * 2 + t // HALF)
                    nc.vector.tensor_reduce(negm[:, t % HALF, :],
                                            ps[:, bank:bank + 2, :].rearrange("p a (c k) -> p (a c) k", k=D), AX,
                                            ALU.max, negate=True).then_inc(s_max, 1)
                    if t % HALF == HALF - 1:
                        n = H * 2 + t // HALF
                        dve.wait_ge(s_max, H * T + t + 1)
                        dve.wait_ge(mt_psum, START + n)
                        nc.vector.tensor_scalar(mhl[:, :, 0:16], negm[:], F16_MAX, -F16_MAX, ALU.min,
                                                ALU.max).then_inc(mhi_ready, 1)
                        dve.wait_ge(mhi_ready, n + 1)
                        nc.vector.tensor_tensor(mhl[:, :, 16:32], negm[:], mhl[:, :, 0:16], ALU.subtract).then_inc(m_ready, 1)

                q_rest(b * NH, 0)
                q_rest(b * NH + 1, 1)
                for t in range(T):
                    maxima(b * NH, t, 4 * (t % 2))

                def head(H, g, j, left):
                    for t in range(T):
                        n = H * T + t
                        w, sw = weighted_sb[t % 2], sumw[j % 2]
                        z = o_ps[:, :, :, D]
                        dve.wait_ge(pv_psum, START + n + 1)
                        nc.vector.reciprocal(places(zinv[:]), z).then_inc(inv_ready, 1)
                        dve.wait_ge(inv_ready, n + 1)
                        nc.vector.tensor_tensor(places(sw[:, t, :]), z, places(zinv[:]), ALU.mult).then_inc(sumw_ready, 1)
                        dve.wait_ge(sumw_ready, n + 1)
                        nc.vector.tensor_tensor(coef[:], sw[:, t, :], zinv[:], ALU.mult).then_inc(coef_ready, 1)
                        dve.wait_ge(coef_ready, n + 1)
                        dve.wait_ge(chunks_summed, n + 1)
                        nc.vector.tensor_tensor(w[:, 12:16, :], o_ps[:, 2, 0:4, 0:D], wide(coef[:, 12:16], D),
                                                ALU.mult).then_inc(weighted_a, 1)
                        nc.vector.tensor_tensor(w[:, 0:6, :], o_ps[:, 0, :, 0:D], wide(coef[:, 0:6], D),
                                                ALU.mult).then_inc(weighted_b, 1)
                        nc.vector.tensor_tensor(w[:, 6:12, :], o_ps[:, 1, :, 0:D], wide(coef[:, 6:12], D),
                                                ALU.mult).then_inc(weighted, 1)
                        if left >= 1:
                            maxima(H + 1, t)
                        if t == HALF and left >= 2:
                            q_rest(H + 2, j % 2)
                        if left == 0 and more:
                            if t == 0:
                                dve.wait_ge(q_psum, START + H + 1)
                            if t < 3:
                                convolve(b + 1, t)
                            if t >= HALF:
                                keys_rest(b + 1, t - HALF)
                    nc.vector.tensor_reduce(total[:, bass.ds(g * REP + j, 1), :].rearrange("p a t -> p (a t)"),
                                            sw[:, :, 0:NCH], AX, ALU.add).then_inc(total_ready, 1)

                each_head(dve, b, head)
                dve.wait_ge(total_ready, (b + 1) * NH)
                nc.vector.tensor_scalar(tinv[:], total[:], 1e-9, None, ALU.add).then_inc(tinv_ready, 1)
                dve.wait_ge(tinv_ready, b * 2 + 1)
                nc.vector.reciprocal(tinv[:], tinv[:]).then_inc(tinv_ready, 1)
                dve.wait_ge(tinv_ready, b * 2 + 2)
                dve.wait_ge(chunks_summed, (b + 1) * NH * T + 2)
                for t in range(T):
                    heads = big2[:, t, :].rearrange("p (h d) -> p h d", d=D)
                    nc.vector.tensor_tensor(heads, heads, wide(tinv[:, :, t], D), ALU.mult).then_inc(att_normed, 1)
                dve.wait_ge(g_ready, START + ((b + 1) * T))
                for t in range(T):
                    dve.wait_ge(y_psum, b * T + t + 1)
                    nc.vector.tensor_tensor(prod[t % 2][:], ps[:, 4 + t % 2, 0:C], g_cur[:, t, :], ALU.mult).then_inc(prod_ready, 1)
                    dve.wait_ge(prod_ready, START + b * T + t + 1)
                    xt = x_sb[:, bass.ds(b * T + t, 1), :].rearrange("p a c -> p (a c)")
                    nc.vector.tensor_tensor(xt, xt, prod[t % 2][:], ALU.add).then_inc(x_ready, 1)

            each_sequence(dve, sequence)

            dve.wait_ge(x_ready, B * T)
            norm_dve(1)
            do(nc.vector.memset(mhl[:], 0.0))
            dve.wait_ge(logits_psum, 1)
            dve.wait_ge(pos_loaded, 16 * 7)
            logits = ps[:, 6, :].rearrange("p (t e) -> p t e", e=E1)
            rb = br1_sb[:].unsqueeze(1).to_broadcast([P, NT, E1])
            row = stat[:, 0, :]
            do(nc.vector.tensor_tensor(rt[0], logits, rb, ALU.add))
            do(nc.vector.tensor_reduce(row, rt[0], AX, ALU.max))
            nc.vector.tensor_tensor(rt[0], rt[0], wide(row, E1), ALU.subtract).then_inc(shifted, 1)
            dve.wait_ge(r_exp, 1)
            do(nc.vector.tensor_reduce(stat[:, 1, :], rt[1], AX, ALU.add))
            do(nc.vector.reciprocal(stat[:, 2, :], stat[:, 1, :]))
            do(nc.vector.tensor_tensor(rt[2], rt[1], wide(stat[:, 2, :], E1), ALU.mult))
            for t in range(NT):
                last = nc.vector.max(top8[:, t, :], rt[2][:, t, :])
            do(last)
            fourth = top8[:, :, 3:4].to_broadcast([P, NT, E1])
            dve.wait_ge(masks_ready, 1)
            do(nc.vector.tensor_tensor(rt[3], rt[2], fourth, ALU.is_gt))
            do(nc.vector.tensor_tensor(rt[4], rt[2], fourth, ALU.is_equal))
            do(nc.vector.tensor_reduce(stat[:, 3, :], rt[3], AX, ALU.add))
            one_dim = lambda ap: ap.rearrange("p t e -> p (t e)")
            do(nc.vector.tensor_tensor_scan(one_dim(rt[5]), one_dim(carry[:]), one_dim(rt[4]), 0.0, ALU.mult, ALU.add))
            do(nc.vector.tensor_tensor(rt[5], rt[5], wide(stat[:, 3, :], E1), ALU.add))
            do(nc.vector.tensor_scalar(rt[6], rt[5], 4.0, None, ALU.is_le))
            do(nc.vector.tensor_tensor(rt[4], rt[4], rt[6], ALU.mult))
            do(nc.vector.tensor_tensor(rt[3], rt[3], rt[4], ALU.add))
            do(nc.vector.tensor_tensor(rt[2], rt[2], rt[3], ALU.mult))
            do(nc.vector.tensor_reduce(stat[:, 1, :], rt[2], AX, ALU.add))
            do(nc.vector.reciprocal(stat[:, 2, :], stat[:, 1, :]))
            nc.vector.tensor_tensor(share[:], rt[2], wide(stat[:, 2, :], E1), ALU.mult).then_inc(share_ready, 1)
            dve.wait_ge(share_ready, 1)
            dve.wait_ge(b2_ready, NT // 4)
            with dve.Fori(0, NT // 4) as k:
                for e in range(E1):
                    dve.wait_ge(down_psum, k * E1 + e + 1)
                    for t in range(4):
                        n = k * E1 * 4 + e * 4 + t
                        whole = gate1[:, bass.ds(k * 4 + t, 1), :].rearrange("p a c -> p (a c)")
                        src = whole if e == 0 else acc[:, t, :]
                        dst = whole if e == E1 - 1 else acc[:, t, :]
                        if e > 0:
                            dve.wait_ge(acc_ready, START + n - 3)
                        nc.vector.scalar_tensor_tensor(
                            out=dst, in0=ps[:, 4 + e % 2, t * C:(t + 1) * C],
                            scalar=share[:, bass.ds(k * 4 + t, 1), e:e + 1].rearrange("p a c -> p (a c)"), in1=src,
                            op0=ALU.mult, op1=ALU.add).then_inc(acc_ready, 1)

            with dve.Fori(0, B) as b:
                nc.vector.tensor_copy(hcur[:], xnt[:, b, 1:S + 1]).then_inc(h1_ready, 1)

                def add_positions(H, i):
                    which, half = PARTS[i]
                    cols = slice(half * BANK, (half + 1) * BANK)
                    dve.wait_ge(qk_psum, START + H * NP + i + 1)
                    dve.wait_ge(qk_ready, NP + H * NP + i - NP + 1)
                    nc.vector.tensor_tensor(qkf[which][:, cols], ps[:, 6, :], pos2[:, cols],
                                            ALU.add).then_inc(qkf_ready, 1)

                def rest(H, p, i):
                    which, half = PARTS[i]
                    cols = slice(half * BANK, (half + 1) * BANK)
                    dve.wait_ge(qk_hi, H * NP + i + 1)
                    if which == 0:
                        nc.vector.scalar_tensor_tensor(out=q2[p][0:D, cols], in0=qkf[0][0:D, cols], scalar=SCALE,
                                                       in1=qhi[p][0:D, cols], op0=ALU.mult,
                                                       op1=ALU.subtract).then_inc(qk_ready, 1)
                    else:
                        nc.vector.tensor_tensor(kst[D:P, p, cols], qkf[1][D:P, cols], kst[D:P, p, cols],
                                                ALU.subtract).then_inc(qk_ready, 1)

                def maxima1(H, t):
                    dve.wait_ge(s1_psum, H * T + t + 1)
                    if t % HALF == 0:
                        dve.wait_ge(m1_ready, START + H * 2 + t // HALF)
                    nc.vector.tensor_reduce(negm1[:, t % HALF, :], s_ps[:, 0:(t + 1) * P], AX, ALU.max,
                                            negate=True).then_inc(s1_max, 1)
                    if t % HALF == HALF - 1:
                        n = H * 2 + t // HALF
                        dve.wait_ge(s1_max, H * T + t + 1)
                        dve.wait_ge(mt1_psum, START + n)
                        nc.vector.tensor_scalar(mhl[:, :, 0:1], negm1[:], F16_MAX, -F16_MAX, ALU.min,
                                                ALU.max).then_inc(mhi1_ready, 1)
                        dve.wait_ge(mhi1_ready, n + 1)
                        nc.vector.tensor_tensor(mhl[:, :, 16:17], negm1[:], mhl[:, :, 0:1],
                                                ALU.subtract).then_inc(m1_ready, 1)

                for i in range(NP + 1):
                    if i < NP:
                        add_positions(b * NH1, i)
                    if i > 0:
                        rest(b * NH1, 0, i - 1)
                for t in range(T):
                    maxima1(b * NH1, t)
                    if t < NP:
                        add_positions(b * NH1 + 1, t)
                    if 1 <= t <= NP:
                        rest(b * NH1 + 1, 1, t - 1)

                def head1(H, h, p, left):
                    for t in range(T):
                        n = H * T + t
                        dve.wait_ge(pv1_psum, START + n + 1)
                        nc.vector.reciprocal(zinv1[:, t:t + 1], ps[:, 4 + t % 2, D:D + 1]).then_inc(inv1_ready, 1)
                        if left >= 1:
                            maxima1(H + 1, t)
                        dve.wait_ge(inv1_ready, n + 1)
                        nc.vector.tensor_scalar(att1[:, t, bass.ds(h * D, D)], ps[:, 4 + t % 2, 0:D], zinv1[:, t:t + 1],
                                                None, ALU.mult).then_inc(att1_ready, 1)
                        if left >= 2:
                            if t < HALF:
                                add_positions(H + 2, t)
                            else:
                                rest(H + 2, p, t - HALF)

                each_head1(dve, b, head1)
                dve.wait_ge(gate1_ready, 1)
                for t in range(T):
                    dve.wait_ge(y1_psum, b * T + t + 1)
                    gt = gate1[:, bass.ds(b * T + t, 1), :].rearrange("p a c -> p (a c)")
                    nc.vector.tensor_tensor(prod[t % 2][:], ps[:, 4 + t % 2, 0:C], gt, ALU.mult).then_inc(prod1_ready, 1)
                    dve.wait_ge(prod1_ready, b * T + t + 1)
                    xt = x_sb[:, bass.ds(b * T + t, 1), :].rearrange("p a c -> p (a c)")
                    nc.vector.tensor_tensor(xt, xt, prod[t % 2][:], ALU.add).then_inc(x1_ready, 1)

        @block.tensor
        def _(pe):
            for started in (q_psum, pv_psum, mt_psum, qk_psum, mt1_psum, pv1_psum):
                pe.nop().then_inc(started, START)
            def norm_pe(L):
                for u in range(B * W1B):
                    pe.wait_ge(normed, L * B + u // W1B + 1)
                    if u >= 2:
                        pe.wait_ge(xt_copied, L * B * W1B + u - 1)
                    for i in range(4):
                        last = nc.tensor.transpose(ps[:, u % 2, i * P:(i + 1) * P], xn[:, u * 4 + i, :], ident[:])
                    last.then_inc(xt_psum, 1)

            pe.wait_ge(ident_ready, 1)
            norm_pe(0)
            pe.wait_ge(weights_loaded, 16 * len(names))
            for u in range(WCOLS // BANK):
                if u >= 2:
                    pe.wait_ge(w_copied, u - 1)
                for i in range(4):
                    k = (u * 4 + i) * P
                    last = nc.tensor.transpose(ps[:, 2 + u % 2, i * P:(i + 1) * P], wraw[:, k:k + P], ident[:])
                last.then_inc(w_psum, 1)
            pe.wait_ge(ctx_ready, 1)
            pe.wait_ge(small_loaded, 16 * 6)
            pe.wait_ge(consts_ready, 1)
            nc.tensor.matmul(ps[0:3, 4, 0:B], kgen_t[:], ctx_mean[:], start=True, stop=True).then_inc(dyn_psum, 1)
            for b in range(B):
                last = nc.tensor.matmul(ps[0:1, 5, b * E0:(b + 1) * E0], ctx_mean[:, b:b + 1], wr0_sb[:],
                                        start=True, stop=True)
            last.then_inc(route_psum, 1)
            pe.wait_ge(sig_ready, 1)
            nc.tensor.matmul(ps[:, 4, 8:8 + B], third[:], sig[:], start=True, stop=True).then_inc(gate_psum, 1)
            pe.wait_ge(wk_ready, 1)
            pe.wait_ge(spread_ready, 1)
            pe.wait_ge(xt_copied, B * W1B)
            pe.wait_ge(w_copied, WCOLS // BANK)
            pe.wait_ge(conv_ready, 1)
            pe.wait_ge(zeros_ready, 1)

            def project_keys(b, kv):
                if kv >= 2:
                    pe.wait_ge(k_ready, b * NKV + kv - 1)
                for i in range(W1B):
                    last = nc.tensor.matmul(ps[:, 2 * (kv % 2) + i, :], wk_dup[:, kv, :],
                                            hcur[:, i * BANK:(i + 1) * BANK], start=True, stop=True)
                last.then_inc(k_psum, 1)

            def project_values(b, i):
                if i >= 1:
                    pe.wait_ge(v_ready, b * NV + i)
                for t in range(2):
                    last = nc.tensor.matmul(ps[:, 7, t * NKV * D:(t + 1) * NKV * D],
                                            hcur[:, (2 * i + t) * P:(2 * i + t + 1) * P],
                                            wt[:, col["v"]:col["v"] + NKV * D], start=True, stop=True)
                last.then_inc(v_psum, 1)

            project_keys(0, 0)
            for i in range(NV):
                if i + 1 < NKV:
                    project_keys(0, i + 1)
                project_values(0, i)

            def sequence(b, more):
                def hidden(units):
                    for u in units:
                        f, half = u // W1B, u % W1B
                        if u >= 2:
                            pe.wait_ge(f1_ready, b * 8 + u - 1)
                        nc.tensor.matmul(ps[:, 4 + u % 2, :], w1e[:, f * P:(f + 1) * P],
                                         xnt[:, b, bass.ds(1 + half * BANK, BANK)], start=True,
                                         stop=True).then_inc(f1_psum, 1)

                def gate_tile(t):
                    if t >= 2:
                        pe.wait_ge(g_ready, START + b * T + t - 1)
                    for f in range(F0 // P):
                        nc.tensor.matmul(ps[:, 2 + t % 2, 0:C], hmid[:, f, t * P:(t + 1) * P], w2e[:, f, :],
                                         start=(f == 0), stop=False)
                    nc.tensor.matmul(ps[:, 2 + t % 2, 0:C], ones_row[:], b2e[:], start=False,
                                     stop=True).then_inc(f2_psum, 1)

                def queries(H, p):
                    pe.wait_ge(wq_ready, H + 1)
                    for i in range(W1B):
                        last = nc.tensor.matmul(ps[:, i, :], wq_dup[p][:], hcur[:, i * BANK:(i + 1) * BANK],
                                                start=True, stop=True)
                    last.then_inc(q_psum, 1)

                def scores(H, g, p, t, bank=0):
                    for i in range(W1B):
                        last = nc.tensor.matmul(ps[:, bank + i, :], qhi[p][:, t * P:(t + 1) * P],
                                                kst[:, g, i * BANK:(i + 1) * BANK], start=True, stop=True)
                    last.then_inc(s_psum, 1)

                def turn_maxima(H, half):
                    pe.wait_ge(m_ready, START + H * 2 + half + 1)
                    pe.wait_ge(mt_ready, START + H * 2 + half)
                    nc.tensor.transpose(mt_ps, mhl[:].rearrange("p a b -> p (a b)"), ident_f16[:]).then_inc(mt_psum, 1)

                def turned_scores(H, g, p, half, units, first=False):
                    for blk in units:
                        u = H * 16 + half * 8 + blk
                        if blk == units[0]:
                            pe.wait_ge(mt_ready, START + H * 2 + half + 1)
                        if not (first and blk < 2):
                            pe.wait_ge(e_ready, u - 1)
                        dst = ps[:, 2 + blk % 2, :]
                        kb = kst[:, g, blk * P:(blk + 1) * P]
                        nc.tensor.matmul(dst, kb, qhi[p][:, half * BANK:(half + 1) * BANK], start=True, stop=False)
                        nc.tensor.matmul(dst, kst2[:, g, blk * P:(blk + 1) * P], q2[p][:, half * BANK:(half + 1) * BANK],
                                         start=False, stop=True).then_inc(st_psum, 1)

                pe.wait_ge(k_ready, (b + 1) * NKV)
                pe.wait_ge(v_ready, (b + 1) * NV)
                queries(b * NH, 0)
                pe.wait_ge(expert_loaded, b * 64 + 64)
                pe.wait_ge(prod_ready, START + b * T)
                hidden(range(4))
                pe.wait_ge(q_ready, b * NH + 1)
                queries(b * NH + 1, 1)
                hidden(range(4, 8))
                pe.wait_ge(q_ready, b * NH + 2)
                pe.wait_ge(f1_ready, b * 8 + 8)
                for t in range(T):
                    if t >= 2:
                        pe.wait_ge(s_max, b * NH * T + t - 1)
                    scores(b * NH, 0, 0, t, 4 * (t % 2))
                    if t < HALF:
                        gate_tile(2 * t)
                        gate_tile(2 * t + 1)
                    if t == HALF:
                        turn_maxima(b * NH, 0)
                        pe.wait_ge(g_ready, START + (b + 1) * T)
                    if t >= HALF:
                        turned_scores(b * NH, 0, 0, 0, (2 * t - 8, 2 * t - 7), first=True)
                pe.wait_ge(s_max, b * NH * T + T)
                pe.nop(nofuse=True)

                def head(H, g, j, left):
                    p = j % 2
                    g_next, p_next = (g, 1 - p) if j < REP - 1 else (g + 1, 1 - p)
                    for t in range(T):
                        n = H * T + t
                        for blk in range(T):
                            if blk == 0:
                                pe.wait_ge(weighted_a, START + n)
                            if blk == 2:
                                pe.wait_ge(weighted_b, START + n)
                            if blk == 5:
                                pe.wait_ge(weighted, START + n)
                            if j == 0 and t == 0 and blk % HALF == 0:
                                pe.wait_ge(vcur_ready, (b * NKV + g) * 2 + blk // HALF + 1)
                            if t % HALF == 0:
                                pe.wait_ge(e_ready, H * 16 + t // HALF * 8 + blk + 1)
                            bank, place = product_place(blk)
                            last = nc.tensor.matmul(ps[:, bank, bass.ds(place * OC, OC)],
                                                    big1[:, t // HALF, blk, bass.ds(t % HALF * P, P)],
                                                    vcur[:, blk, :], start=True, stop=True)
                        last.then_inc(pv_psum, 1)
                        if t == 0:
                            turn_maxima(H, 1)
                        if t == HALF and left >= 1:
                            turn_maxima(H + 1, 0)
                        if left >= 1:
                            if t == HALF + 1 and left >= 2:
                                pe.wait_ge(q_ready, H + 3)
                            pe.wait_ge(s_max, (H + 1) * T + t)
                            scores(H + 1, g_next, p_next, t)
                        if t < HALF:
                            turned_scores(H, g, p, 1, (2 * t, 2 * t + 1))
                        elif left >= 1:
                            turned_scores(H + 1, g_next, p_next, 0, (2 * t - 8, 2 * t - 7))
                        if left == 0 and more and t >= HALF - 1:
                            kv = t - HALF + 1
                            if kv == 0:
                                pe.wait_ge(conv_ready, b + 2)
                                pe.wait_ge(s_max, (b + 1) * NH * T)
                            if kv == 1:
                                pe.wait_ge(mt_ready, START + (b + 1) * NH * 2)
                            if kv < NKV:
                                project_keys(b + 1, kv)
                            if kv >= 1:
                                project_values(b + 1, kv - 1)
                        if t == HALF and left >= 2:
                            pe.wait_ge(s_max, (H + 1) * T + t + 1)
                            queries(H + 2, p)

                each_head(pe, b, head)

                def turn_output(t):
                    pe.wait_ge(att_normed, b * T + t + 1)
                    if t >= 2:
                        pe.wait_ge(at_ready, b * T + t - 1)
                    for f in range(8):
                        last = nc.tensor.transpose(ps[:, 2 * (t % 2) + f // 4, bass.ds(f % 4 * P, P)],
                                                   big2[:, t, f * P:(f + 1) * P], ident[:])
                    last.then_inc(at_psum, 1)

                turn_output(0)
                for t in range(T):
                    if t + 1 < T:
                        turn_output(t + 1)
                    if t >= 2:
                        pe.wait_ge(prod_ready, START + b * T + t - 1)
                    pe.wait_ge(at_ready, b * T + t + 1)
                    for f in range(8):
                        last = nc.tensor.matmul(ps[:, 4 + t % 2, 0:C], att_t[t % 2][:, f, :],
                                                wt[:, col["o"] + f * P:col["o"] + (f + 1) * P],
                                                start=(f == 0), stop=(f == 7))
                    last.then_inc(y_psum, 1)

            each_sequence(pe, sequence)

            norm_pe(1)
            pe.wait_ge(xt_copied, 2 * B * W1B)
            pe.wait_ge(pos_loaded, 16 * 7)
            tile = lambda n: xnt[:, n // T, 1 + n % T * P:1 + (n % T + 1) * P]
            for n in range(NT):
                last = nc.tensor.matmul(ps[:, 6, n * E1:(n + 1) * E1], tile(n), wr1_sb[:], start=True, stop=True)
            last.then_inc(logits_psum, 1)
            pe.wait_ge(share_ready, 1)
            for u in range(NT // 4):
                if u >= 2:
                    pe.wait_ge(ct_ready, u - 1)
                for i in range(4):
                    last = nc.tensor.transpose(ps[0:E1, u % 2, i * P:(i + 1) * P], share[:, 4 * u + i, :], ident[:])
                last.then_inc(ct_psum, 1)
                pe.wait_ge(ct_ready, u + 1)
                if u >= 2:
                    pe.wait_ge(b2_ready, u - 1)
                for i in range(4):
                    last = nc.tensor.matmul(ps[:, 2 + u % 2, i * P:(i + 1) * P], att_t[u % 2][0:E1, i, :], b2_sb[:],
                                            start=True, stop=True)
                last.then_inc(b2_psum, 1)
            pe.wait_ge(b2_ready, NT // 4)
            pe.wait_ge(experts_loaded, 16 * 3)
            with pe.Fori(0, B) as b, pe.Fori(0, W1B) as half:
                k = b * W1B + half
                chunk = xnt[:, b, bass.ds(1 + half * BANK, BANK)]

                def up(e):
                    for f in range(F1 // P):
                        u = k * E1 * 2 + e * 2 + f
                        if e >= 2:
                            pe.wait_ge(up_ready, u - 3)
                        nc.tensor.matmul(ps[:, 2 * (e % 2) + f, :], up_w[:, e, f * P:(f + 1) * P], chunk,
                                         start=True, stop=True).then_inc(up_psum, 1)

                def down(e):
                    n = k * E1 + e
                    pe.wait_ge(up_ready, n * 2 + 2)
                    if e >= 2:
                        pe.wait_ge(acc_ready, START + n * 4 - 4)
                    for t in range(4):
                        for f in range(F1 // P):
                            last = nc.tensor.matmul(ps[:, 4 + e % 2, t * C:(t + 1) * C],
                                                    mid1[:, e % 4, f, t * P:(t + 1) * P], down_w[:, e, f, :],
                                                    start=(f == 0), stop=(f == F1 // P - 1))
                    last.then_inc(down_psum, 1)

                pe.wait_ge(acc_ready, START + k * E1 * 4)
                up(0)
                for e in range(E1):
                    if e + 1 < E1:
                        up(e + 1)
                    down(e)

            pe.wait_ge(ones_ready, 1)
            pe.wait_ge(acc_ready, START + NT // 4 * E1 * 4)
            with pe.Fori(0, B) as b:
                pe.wait_ge(h1_ready, b + 1)
                for t in range(T):
                    if t >= 2:
                        pe.wait_ge(v1_ready, b * T + t - 1)
                    wv = wt[:, col["qkv"]:col["qkv"] + NH1 * 3 * D].rearrange("p (h d) -> p h d", h=NH1)
                    nc.tensor.matmul(ps[:, 4 + t % 2, :], hcur[:, t * P:(t + 1) * P], wv[:, :, 2 * D:3 * D],
                                     start=True, stop=True).then_inc(v1_psum, 1)

                def project(H, p, i):
                    which, half = PARTS[i]
                    if i == 0:
                        pe.wait_ge(w1_ready, H + 1)
                    pe.wait_ge(qkf_ready, START + H * NP + i)
                    nc.tensor.matmul(ps[:, 6, :], wq_dup[p][:] if which == 0 else wk_dup[:, p, :],
                                     hcur[:, half * BANK:(half + 1) * BANK], start=True, stop=True).then_inc(qk_psum, 1)

                def scores1(H, p, t, wait):
                    if wait:
                        pe.wait_ge(s1_max, H * T + t)
                    last_bank = t * P // BANK
                    for c in range(last_bank + 1):
                        n = min(BANK, (t + 1) * P - c * BANK)
                        last = nc.tensor.matmul(ps[:, c, 0:n], qhi[p][:, t * P:(t + 1) * P],
                                                kst[:, p, c * BANK:c * BANK + n], start=True, stop=(c < last_bank))
                    d = t * P % BANK
                    nc.tensor.matmul(ps[:, last_bank, d:d + P], ident_h[:], mask_qk[:], start=False,
                                     stop=True).then_inc(s1_psum, 1)

                def turn_maxima1(H, half):
                    pe.wait_ge(m1_ready, START + H * 2 + half + 1)
                    pe.wait_ge(mt1_ready, START + H * 2 + half)
                    nc.tensor.transpose(mt_ps, mhl[:].rearrange("p a b -> p (a b)"), ident_f16[:]).then_inc(mt1_psum, 1)

                def turned_scores1(H, p, units, first=False):
                    for half, blk in units:
                        u = H * NU + unit_index(half, blk)
                        c0 = unit_cols(half, blk)
                        if blk == 0 or (half, blk) == units[0]:
                            pe.wait_ge(mt1_ready, START + H * 2 + half + 1)
                        if not (first and blk < 2):
                            pe.wait_ge(e_ready1, u - 1)
                        dst = ps[:, 2 + blk % 2, c0:BANK]
                        kb = kst[:, p, blk * P:(blk + 1) * P]
                        q0 = half * BANK + c0
                        nc.tensor.matmul(dst, kb, qhi[p][:, q0:(half + 1) * BANK], start=True, stop=False)
                        last = nc.tensor.matmul(dst, kst2[:, p, blk * P:(blk + 1) * P], q2[p][:, q0:(half + 1) * BANK],
                                                start=False, stop=(blk < half * HALF))
                        if blk >= half * HALF:
                            last = nc.tensor.matmul(ps[:, 2 + blk % 2, c0:c0 + P], ident_h[:], mask_kq[:],
                                                    start=False, stop=True)
                        last.then_inc(st_psum1, 1)

                pe.wait_ge(v1_ready, (b + 1) * T)
                for i in range(NP):
                    project(b * NH1, 0, i)
                for t in range(T):
                    if t % HALF == 0:
                        pe.wait_ge(qk_ready, NP + b * NH1 * NP + (2 if t == 0 else NP))
                    scores1(b * NH1, 0, t, t > 0)
                    if t < NP:
                        project(b * NH1 + 1, 1, t)
                    if t == HALF - 1:
                        turn_maxima1(b * NH1, 0)
                    if t >= HALF:
                        turned_scores1(b * NH1, 0, UNITS[0][t - HALF:t - HALF + 1], first=True)

                def head1(H, h, p, left):
                    for t in range(T):
                        n = H * T + t
                        half = t // HALF
                        pe.wait_ge(att1_ready, START + (n - 1 if t > 0 else n))
                        for blk in range(t + 1):
                            if t % HALF == 0:
                                pe.wait_ge(e_ready1, H * NU + unit_index(half, blk) + 1)
                            if t % HALF != 0 and blk == t:
                                pe.wait_ge(e_ready1, H * NU + unit_index(half, blk) + 1)
                            last = nc.tensor.matmul(ps[:, 4 + t % 2, 0:D + 1],
                                                    big1[:, half, blk, bass.ds(t % HALF * P, P)],
                                                    v1[:, bass.ds(h, 1), blk, :].rearrange("p a c -> p (a c)"),
                                                    start=(blk == 0), stop=(blk == t))
                        last.then_inc(pv1_psum, 1)
                        if t == 0:
                            turn_maxima1(H, 1)
                        if left >= 1:
                            if t == HALF:
                                turn_maxima1(H + 1, 0)
                            if t % HALF == 0:
                                pe.wait_ge(qk_ready, NP + (H + 1) * NP + (2 if t == 0 else NP))
                            scores1(H + 1, 1 - p, t, True)
                        if t < HALF and left >= 2:
                            project(H + 2, p, t)
                        if t < HALF:
                            turned_scores1(H, p, UNITS[1][2 * t:2 * t + 2])
                        elif left >= 1:
                            turned_scores1(H + 1, 1 - p, UNITS[0][t - HALF:t - HALF + 1])

                each_head1(pe, b, head1)

                def turn_output1(t):
                    if t == 0:
                        pe.wait_ge(att1_ready, START + ((b + 1) * NH1 * T))
                    if t >= 2:
                        pe.wait_ge(at1_ready, b * T + t - 1)
                    for f in range(4):
                        last = nc.tensor.transpose(ps[:, t % 2, f * P:(f + 1) * P], att1[:, t, f * P:(f + 1) * P], ident[:])
                    last.then_inc(at1_psum, 1)

                turn_output1(0)
                for t in range(T):
                    if t + 1 < T:
                        turn_output1(t + 1)
                    if t >= 2:
                        pe.wait_ge(prod1_ready, b * T + t - 1)
                    pe.wait_ge(at1_ready, b * T + t + 1)
                    for f in range(4):
                        last = nc.tensor.matmul(ps[:, 4 + t % 2, 0:C], att_t[t % 2][:, f, :],
                                                wt[:, col["o1"] + f * P:col["o1"] + (f + 1) * P],
                                                start=(f == 0), stop=(f == 3))
                    last.then_inc(y1_psum, 1)


_INS = ['L0_attn_hidden_states', 'L0_attn_w_q', 'L0_attn_w_k', 'L0_attn_w_v', 'L0_attn_w_o', 'L0_attn_w_kgen',
        'L0_attn_b_kgen', 'L0_attn_w_conv', 'L0_attn_b_conv', 'L0_ffn_Wr', 'L0_ffn_br', 'L0_ffn_W1', 'L0_ffn_b1',
        'L0_ffn_W2', 'L0_ffn_b2', 'L1_attn_Wqkv', 'L1_attn_Wo', 'L1_ffn_router_w', 'L1_ffn_router_b', 'L1_ffn_w1',
        'L1_ffn_b1', 'L1_ffn_w2', 'L1_ffn_b2']


def position_table(seq, dim):
    pos = np.arange(seq, dtype=np.float32)[:, None]
    div = np.exp(np.arange(0, dim, 2, dtype=np.float32) * np.float32(-np.log(10000.0) / dim))
    ang = pos * div
    return np.ascontiguousarray(np.stack([np.sin(ang), np.cos(ang)], axis=-1).reshape(seq, dim).T.astype(np.float32))


def kernel(**inputs):
    import concourse.bacc as _bacc
    from concourse.bass_utils import run_bass_kernel_spmd as _run

    nc = _bacc.Bacc("TRN2", target_bir_lowering=False, num_devices=1)
    arrays = {f"in_{name}": np.ascontiguousarray(inputs[name]) for name in _INS}
    seq = inputs['L0_attn_hidden_states'].shape[1]
    arrays["in_positions"] = position_table(seq, 64)
    args = [nc.dram_tensor(n, a.shape, mybir.dt.from_np(a.dtype), kind="ExternalInput").ap()
            for n, a in arrays.items()]
    shape = inputs['L0_attn_hidden_states'].shape
    args.append(nc.dram_tensor("out_x", shape, F32, kind="ExternalOutput").ap())
    gated_layers(nc, *args)
    r = _run(nc, [arrays], core_ids=[0])
    return r.results[0]["out_x"]
```

```python
from contextlib import ExitStack

import numpy as np

import concourse.bass as bass
from concourse import mybir

F32, BF16, F16, U32 = (mybir.dt.float32, mybir.dt.bfloat16, mybir.dt.float16, mybir.dt.uint32)
ALU = mybir.AluOpType
ACT = mybir.ActivationFunctionType
AX = mybir.AxisListType.X
P = 128
BANK = 512
START = 1
PLACES = 2
EPS = 1e-5


def gated_layers(nc, x_in, w_q, w_k, w_v, w_o, w_kgen, b_kgen, w_conv, b_conv,
                 wr0, br0, w1_0, b1_0, w2_0, b2_0, w_qkv, w_o1, wr1, br1, w1_1, b1_1, w2_1, b2_1,
                 pos_t, out):
    B, S, C = x_in.shape
    D = 64
    NH = w_q.shape[0] // D
    NKV = w_k.shape[0] // D
    REP = NH // NKV
    T = S // P
    NT = B * T
    HALF = T // 2
    NCH = S // D
    OC = 2 * (D + 1)
    NS = 18
    E0, F0 = wr0.shape[1], w1_0.shape[2]
    E1, F1 = wr1.shape[1], w1_1.shape[2]
    NH1 = w_o1.shape[1] // D
    SCALE = float(D) ** -0.5
    MASKED = -1e30
    F16_MAX = 65504.0

    names = [("q", w_q), ("k", w_k), ("v", w_v), ("o", w_o), ("qkv", w_qkv), ("o1", w_o1)]
    col, n = {}, 0
    for name, w in names:
        col[name] = n
        n += w.shape[0] * w.shape[1] // C
    WCOLS = n

    ctx = ExitStack()
    with ctx:
        def sb(name, shape, dt=F32):
            return ctx.enter_context(nc.sbuf_tensor(name, shape, dt))

        def sem(name):
            return ctx.enter_context(nc.semaphore(name))

        ps = ctx.enter_context(nc.psum_tensor("ps", [P, 8, BANK], F32))
        x_sb = sb("x_sb", [P, NT, C])
        xnt = sb("xnt", [P, B, S + 2])
        big1 = sb("big1", [P, 2, 8, BANK])
        big2 = sb("big2", [P, T, NH * D])
        wt = sb("wt", [P, WCOLS])
        hcur = sb("hcur", [P, S])
        g_cur = sb("g_cur", [P, T, C])
        kst = sb("kst", [P, NKV, S], F16)
        kst2 = sb("kst2", [P, NKV, S], F16)
        vbd = sb("vbd", [P, NKV, T, OC])
        qhi = [sb(f"qhi{i}", [P, S], F16) for i in range(2)]
        q2 = [sb(f"q2{i}", [P, S], F16) for i in range(2)]
        wq_dup = [sb(f"wq_dup{i}", [P, P]) for i in range(2)]
        wk_dup = sb("wk_dup", [P, NKV, P])
        weighted_sb = [sb(f"weighted{i}", [P, NCH, D]) for i in range(2)]
        ident = sb("ident", [P, P])
        ident_h = sb("ident_h", [P, P], BF16)
        row_chunk = sb("row_chunk", [P, 16])
        ident_f16 = sb("ident_f16", [P, P], F16)
        negm = sb("negm", [P, HALF, 16])
        mhl = sb("mhl", [P, HALF, 32], F16)
        zinv = sb("zinv", [P, NS])
        coef = sb("coef", [P, NS])
        sumw = [sb(f"sumw{i}", [P, T, NS]) for i in range(2)]
        total = sb("total", [P, NH, T])
        tinv = sb("tinv", [P, NH, T])
        att_t = [sb(f"att_t{i}", [P, 8, P]) for i in range(2)]
        prod = [sb(f"prod{i}", [P, C]) for i in range(2)]
        stat = sb("stat", [P, 4, NT])
        ctx_mean = sb("ctx_mean", [P, B])
        kgen_t = sb("kgen_t", [P, 3])
        bkgen = sb("bkgen", [3, 1])
        sig = sb("sig", [3, B])
        third = sb("third", [3, P])
        gate = sb("gate", [P, B])
        conv_w = sb("conv_w", [P, 3])
        conv_b = sb("conv_b", [P, 1])
        conv_wg = sb("conv_wg", [P, B, 4])
        wr0_sb = sb("wr0_sb", [P, E0])
        br0_sb = sb("br0_sb", [1, E0])
        route = sb("route", [1, B, E0])
        route_max = sb("route_max", [1, B, 8])
        route_idx = sb("route_idx", [1, B, 8], U32)
        w1e = sb("w1e", [P, F0])
        w2e = sb("w2e", [P, F0 // P, C])
        b1e = sb("b1e", [P, F0 // P])
        b2e = sb("b2e", [1, C])
        ones_row = sb("ones_row", [1, P])
        vcur = sb("vcur", [P, T, OC])
        pos2 = vcur[:].rearrange("p t c -> p (t c)")[:, 0:S]
        mask_qk = sb("mask_qk", [P, P], BF16)
        mask_kq = sb("mask_kq", [P, P], BF16)
        negm1 = sb("negm1", [P, HALF, 1])
        zinv1 = sb("zinv1", [P, T])
        wr1_sb = sb("wr1_sb", [P, E1])
        br1_sb = sb("br1_sb", [P, E1])
        b1_sb = sb("b1_sb", [P, F1 // P, E1])
        b2_sb = sb("b2_sb", [E1, C])
        share = sb("share", [P, NT, E1])
        carry = sb("carry", [P, NT, E1])
        top8 = sb("top8", [P, NT, 8])
        acc = sb("acc", [P, 4, C])


        def named(*names):
            return [sem(name) for name in names]

        x_loaded = [sem(f"x_loaded{b}") for b in range(B)]
        weights_loaded, small_loaded, expert_loaded, stored = named(
            "weights_loaded", "small_loaded", "expert_loaded", "stored")
        ident_ready, pool_step, consts_ready, spread_ready, zeros_ready = named(
            "ident_ready", "pool_step", "consts_ready", "spread_ready", "zeros_ready")
        w_psum, w_copied = named("w_psum", "w_copied")
        dve_step, centered, squared, var_ready, std_ready, normed, xt_psum, xt_copied = named(
            "dve_step", "centered", "squared", "var_ready", "std_ready", "normed", "xt_psum", "xt_copied")
        ctx_ready, dyn_psum, sig_ready, gate_psum, route_psum, route_ready = named(
            "ctx_ready", "dyn_psum", "sig_ready", "gate_psum", "route_psum", "route_ready")
        conv_ready, conv_step = named("conv_ready", "conv_step")
        f1_psum, f1_ready, f2_psum, g_ready = named("f1_psum", "f1_ready", "f2_psum", "g_ready")
        wk_ready, k_psum, k_hi, k_ready, v_psum, v_ready, vcur_ready, wq_ready, q_psum, q_hi, q_ready = named(
            "wk_ready", "k_psum", "k_hi", "k_ready", "v_psum", "v_ready", "vcur_ready", "wq_ready", "q_psum", "q_hi",
            "q_ready")
        s_psum, s_max, mhi_ready, m_ready, mt_psum, mt_ready = named(
            "s_psum", "s_max", "mhi_ready", "m_ready", "mt_psum", "mt_ready")
        st_psum, e_ready, pv_psum, inv_ready, sumw_ready, coef_ready, weighted_a, weighted_b, weighted = named(
            "st_psum", "e_ready", "pv_psum", "inv_ready", "sumw_ready", "coef_ready", "weighted_a",
            "weighted_b", "weighted")
        tree_step, chunks_summed, total_ready = named("tree_step", "chunks_summed", "total_ready")
        tinv_ready, att_normed, at_psum, at_ready, y_psum, prod_ready, x_ready = named(
            "tinv_ready", "att_normed", "at_psum", "at_ready", "y_psum", "prod_ready", "x_ready")

        logits_psum, shifted, r_exp, share_ready, st_psum1, e_ready1 = named(
            "logits_psum", "shifted", "r_exp", "share_ready", "st_psum1", "e_ready1")
        ct_psum, ct_ready, b2_psum, b2_ready, experts_loaded = named(
            "ct_psum", "ct_ready", "b2_psum", "b2_ready", "experts_loaded")
        x_hi_ready, x_lo_ready, w_hi_ready, w_lo_ready, mid_hi_ready, mid_lo_ready = named(
            "x_hi_ready", "x_lo_ready", "w_hi_ready", "w_lo_ready", "mid_hi_ready", "mid_lo_ready")
        up_psum, up_ready, down_psum, acc_ready, gate1_ready, pos_loaded, ones_ready, masks_ready = named(
            "up_psum", "up_ready", "down_psum", "acc_ready", "gate1_ready", "pos_loaded", "ones_ready",
            "masks_ready")
        h1_ready, v1_psum, v1_ready, w1_ready, qk_psum, qkf_ready, qk_hi, qk_ready = named(
            "h1_ready", "v1_psum", "v1_ready", "w1_ready", "qk_psum", "qkf_ready", "qk_hi", "qk_ready")
        s1_psum, s1_max, mhi1_ready, m1_ready, mt1_psum, mt1_ready, pv1_psum, inv1_ready, att1_ready = named(
            "s1_psum", "s1_max", "mhi1_ready", "m1_ready", "mt1_psum", "mt1_ready", "pv1_psum", "inv1_ready",
            "att1_ready")
        at1_psum, at1_ready, y1_psum, prod1_ready, x1_ready = named(
            "at1_psum", "at1_ready", "y1_psum", "prod1_ready", "x1_ready")

        flat1 = big1[:].rearrange("p a b c -> p (a b c)")
        flat2 = big2[:].rearrange("p a b -> p (a b)")
        up_w = flat1[:, 0:E1 * F1].rearrange("p (e f) -> p e f", e=E1)
        down_w = flat1[:, E1 * F1:2 * E1 * F1].rearrange("p (e f c) -> p e f c", e=E1, f=F1 // P)
        gate1 = flat2[:, 0:NT * C].rearrange("p (t c) -> p t c", c=C)
        att1 = flat2[:, NT * C:NT * C + T * NH1 * D].rearrange("p (t f) -> p t f", t=T)
        FN = F1 // P * BANK
        mid1 = flat2[:, NT * C:NT * C + 2 * FN].rearrange("p (a f t) -> p a f t", a=2, f=F1 // P)
        mid_hi, mid_lo = [flat2[:, NT * C + (2 + i) * FN:NT * C + (3 + i) * FN].bitcast(F16)
                          .rearrange("p (a f t) -> p a f t", a=2, f=F1 // P) for i in range(2)]
        halves = vbd[:].rearrange("p k t c -> p (k t c)").bitcast(F16)
        up_hi = halves[:, 0:E1 * F1].rearrange("p (e f) -> p e f", e=E1)
        down_hi = halves[:, E1 * F1:2 * E1 * F1].rearrange("p (e f c) -> p e f c", e=E1, f=F1 // P)
        x_hi = kst[:].rearrange("p b s -> p (b s)")
        x_lo = kst2[:].rearrange("p b s -> p (b s)")
        room = [weighted_sb[0][:].rearrange("p a b -> p (a b)").bitcast(F16),
                weighted_sb[1][:].rearrange("p a b -> p (a b)").bitcast(F16), hcur[:].bitcast(F16), qhi[0][:], qhi[1][:]]
        UP_LO = [(room[0], 0, E1 // 2), (room[1], E1 // 2, E1 // 2)]
        DOWN_LO = [(room[2], 0, E1 // 2), (room[3], E1 // 2, E1 // 4), (room[4], 3 * E1 // 4, E1 // 4)]

        def lesser(table, e):
            for place, first, count in table:
                if first <= e < first + count:
                    return place[:, (e - first) * F1:(e - first + 1) * F1]
        rt = [flat2[:, NT * C + i * BANK:NT * C + (i + 1) * BANK].rearrange("p (t e) -> p t e", e=E1)
              for i in range(7)]
        qkf = [w[:].rearrange("p a b -> p (a b)") for w in weighted_sb]
        v1 = vbd[:].rearrange("p k t c -> p (k t c)").rearrange("p (h t c) -> p h t c", h=NH1, t=T)
        NU = HALF + T
        LATE = [range(0, 0), range(0, 3), range(3, 6), range(6, 8)]
        EARLY = [range(0, 0), range(0, 3), range(3, 5), range(5, 8)]
        EARLY1 = [range(0, 0), range(0, 1), range(1, 2), range(2, 4)]
        UNIT_BANK = [[2, 3, 7, 2, 3, 2, 3, 2], [2, 3, 7, 2, 3, 7, 2, 3]]
        UNIT_BEFORE = [[None, None, None, 0, 2, 3, 4, 5], [None, None, None, 0, 1, 2, 3, 4]]
        QUERY_TILES = (HALF - 1, HALF + 2)
        PARTS = [(0, 0), (1, 0), (0, 1), (1, 1)]
        NP = len(PARTS)
        PART_TILES = (0, 1, 2, HALF)
        NV = T // 2
        UNITS = [[(0, blk) for blk in range(HALF)], [(1, blk) for blk in range(T)]]

        xn = big1[:].rearrange("p a b c -> p (a b c)")[:, 0:NT * C].rearrange("p (t c) -> p t c", c=C)
        sq = big1[:].rearrange("p a b c -> p (a b c)")[:, NT * C:2 * NT * C].rearrange("p (t c) -> p t c", c=C)
        wraw = big2[:].rearrange("p a b -> p (a b)")[:, 0:WCOLS]
        hmid = big2[:].rearrange("p a b -> p (a b)")[:, 0:F0 // P * S].rearrange("p (f t) -> p f t", f=F0 // P)
        q_whole = [acc[:].rearrange("p a b -> p (a b)"), share[:].rearrange("p a b -> p (a b)")]
        MROWS = slice(D, D + 32)
        mt_ps = ps[:, 7, :].bitcast(F16)[:, 0:P]
        o_ps = ps[:, 4:7, 0:3 * OC].rearrange("p a (b c) -> p a b c", c=D + 1)
        s_ps = ps[:, 0:2, :].rearrange("p a b -> p (a b)")
        W1B = S // BANK

        def wide(ap, n):
            shape = list(ap.shape) + [n]
            return ap.unsqueeze(len(ap.shape)).to_broadcast(shape)

        def product_place(blk):
            return (6, blk) if blk < 2 else (4 + (blk - 2) // 3, (blk - 2) % 3)

        def places(ap):
            return ap.rearrange("p (a b) -> p a b", a=3)

        def chain(signal, ins, eng, tally):
            tally[0] += 1
            ins.then_inc(signal, 1)
            eng.wait_ge(signal, tally[0])

        def each_head(eng, b, do):
            with eng.Fori(0, NKV - 1) as g:
                for j in range(REP):
                    do(b * NH + g * REP + j, g, j, 3)
            for j in range(REP):
                do(b * NH + (NKV - 1) * REP + j, NKV - 1, j, REP - 1 - j)

        def each_sequence(eng, do):
            with eng.Fori(0, B - 1) as b:
                do(b, True)
            do(B - 1, False)

        def each_head1(eng, b, do):
            with eng.Fori(0, NH1 // 2 - 1) as g:
                for p in range(2):
                    do(b * NH1 + g * 2 + p, g * 2 + p, p, 3)
            for p in range(2):
                do(b * NH1 + NH1 - 2 + p, NH1 - 2 + p, p, 1 - p)

        def unit_index(half, blk):
            return half * HALF + blk

        def unit_bank1(half, blk):
            return (2, 3, 7)[unit_index(half, blk) % 3]

        def unit_cols(half, blk):
            return max(0, blk - half * HALF) * P

        block = ctx.enter_context(nc.Block())

        @block.sync
        def _(sp):
            for b in range(B):
                sp.dma_start(x_sb[:, b * T:(b + 1) * T, :],
                             x_in[b].rearrange("(t p) c -> p t c", p=P)).then_inc(x_loaded[b], 16)
            for name, w in names:
                dst = wraw[:, col[name]:col[name] + w.shape[0] * w.shape[1] // C]
                if w.shape[1] == C:
                    sp.dma_start(dst.rearrange("p (n c) -> p n c", c=C),
                                 w.rearrange("(n p) c -> p n c", p=P)).then_inc(weights_loaded, 16)
                else:
                    sp.dma_start(dst, w).then_inc(weights_loaded, 16)
            sp.dma_start(kgen_t[:], w_kgen.rearrange("k c -> c k"),
                         allow_slow_non_contiguous=True).then_inc(small_loaded, 16)
            sp.dma_start(bkgen[:], b_kgen.rearrange("(k a) -> k a", a=1)).then_inc(small_loaded, 16)
            sp.dma_start(conv_w[:], w_conv.rearrange("c a k -> c (a k)")).then_inc(small_loaded, 16)
            sp.dma_start(conv_b[:], b_conv.rearrange("(c a) -> c a", a=1)).then_inc(small_loaded, 16)
            sp.dma_start(wr0_sb[:], wr0).then_inc(small_loaded, 16)
            sp.dma_start(br0_sb[:], br0.rearrange("(a e) -> a e", a=1)).then_inc(small_loaded, 16)
            sp.dma_start(wr1_sb[:], wr1).then_inc(pos_loaded, 16)
            sp.dma_start(br1_sb[:], br1.rearrange("(a e) -> a e", a=1).to_broadcast([P, E1])).then_inc(pos_loaded, 16)
            sp.dma_start(b2_sb[:], b2_1).then_inc(pos_loaded, 16)
            for f in range(F1 // P):
                sp.dma_start(b1_sb[:, f, :], b1_1[:, f * P:(f + 1) * P].rearrange("e p -> p e"),
                             allow_slow_non_contiguous=True).then_inc(pos_loaded, 16)
            sp.wait_ge(route_ready, 1)
            with sp.Fori(0, B) as b:
                sp.wait_ge(g_ready, START + b * T)
                e = sp.value_load(route_idx[0:1, b, 0:1], min_val=0, max_val=E0 - 1)
                sp.dma_start(w1e[:], w1_0[e]).then_inc(expert_loaded, 16)
                sp.dma_start(w2e[:], w2_0[e].rearrange("(n p) c -> p n c", p=P)).then_inc(expert_loaded, 16)
                sp.dma_start(b1e[:], b1_0[e].rearrange("(n p) -> p n", p=P),
                             allow_slow_non_contiguous=True).then_inc(expert_loaded, 16)
                sp.dma_start(b2e[:], b2_0[e].rearrange("(a c) -> a c", a=1)).then_inc(expert_loaded, 16)
            sp.wait_ge(x_ready, B * T)
            sp.dma_start(pos2[0:D, :], pos_t).then_inc(pos_loaded, 16)
            sp.dma_start(pos2[D:P, :], pos_t).then_inc(pos_loaded, 16)
            sp.wait_ge(xt_psum, 2 * B * W1B)
            sp.dma_start(up_w, w1_1.rearrange("e c f -> c e f")).then_inc(experts_loaded, 16)
            for f in range(F1 // P):
                sp.dma_start(down_w[:, :, f, :], w2_1[:, f * P:(f + 1) * P, :].rearrange("e p c -> p e c")).then_inc(experts_loaded, 16)
            for b in range(B):
                sp.wait_ge(x1_ready, (b + 1) * T)
                sp.dma_start(out[b].rearrange("(t p) c -> p t c", p=P),
                             x_sb[:, b * T:(b + 1) * T, :]).then_inc(stored, 16)
            sp.wait_ge(stored, 16 * B)

        @block.gpsimd
        def _(pool):
            step = [0]
            chain(pool_step, nc.gpsimd.memset(ident[:], 0.0), pool, step)
            nc.gpsimd.affine_select(out=ident[:], in_=ident[:], compare_op=ALU.not_equal, fill=1.0, base=0,
                                    pattern=[[-1, P]], channel_multiplier=1).then_inc(ident_ready, 1)
            nc.gpsimd.memset(xnt[:, :, 0:1], 0.0)
            nc.gpsimd.memset(xnt[:, :, S + 1:S + 2], 0.0)
            nc.gpsimd.memset(third[:], 1.0 / 3.0)
            nc.gpsimd.memset(ones_row[:], 1.0).then_inc(consts_ready, 1)
            chain(pool_step, nc.gpsimd.memset(vbd[:], 0.0), pool, step)
            nc.gpsimd.memset(vbd[0:D, :, :, D:D + 1], 1.0)
            chain(pool_step, nc.gpsimd.memset(vbd[D:P, :, :, OC - 1:OC], 1.0), pool, step)
            nc.gpsimd.memset(kst2[:], 0.0)
            nc.gpsimd.memset(q2[0][:], 0.0)
            nc.gpsimd.memset(q2[1][:], 0.0).then_inc(zeros_ready, 1)
            chain(pool_step, nc.gpsimd.memset(mask_qk[:], 0.0), pool, step)
            chain(pool_step, nc.gpsimd.memset(mask_kq[:], 0.0), pool, step)
            nc.gpsimd.affine_select(out=mask_qk[:], in_=mask_qk[:], compare_op=ALU.is_ge, fill=MASKED, base=0,
                                    pattern=[[-1, P]], channel_multiplier=1)
            nc.gpsimd.affine_select(out=mask_kq[:], in_=mask_kq[:], compare_op=ALU.is_ge, fill=MASKED, base=0,
                                    pattern=[[1, P]], channel_multiplier=-1)
            chain(pool_step, nc.gpsimd.memset(carry[:], 1.0), pool, step)
            nc.gpsimd.memset(carry[:, :, 0:1], 0.0).then_inc(masks_ready, 1)
            pool.nop().then_inc(q_ready, W1B)
            pool.nop().then_inc(chunks_summed, 2)
            pool.wait_ge(w_copied, WCOLS // BANK)
            for kv in range(NKV):
                wk = wt[:, col["k"] + kv * D:col["k"] + (kv + 1) * D]
                nc.gpsimd.tensor_copy(wk_dup[:, kv, 0:D], wk)
                last = nc.gpsimd.tensor_copy(wk_dup[:, kv, D:P], wk)
            last.then_inc(wk_ready, 1)

            def stage_wq(H, g, j, p):
                pool.nop(nofuse=True)
                src = wt[:, bass.ds(col["q"] + g * REP * D + j * D, D)]
                nc.gpsimd.tensor_copy(wq_dup[p][:, 0:D], src)
                nc.gpsimd.tensor_copy(wq_dup[p][:, D:P], src).then_inc(wq_ready, 1)

            def sequence(b, more):
                pool.wait_ge(q_psum, START + b * NH * W1B)
                stage_wq(b * NH, 0, 0, 0)
                stage_wq(b * NH + 1, 0, 1, 1)

                def q_rest(H, p, i):
                    cols = slice(i * BANK, (i + 1) * BANK)
                    pool.wait_ge(q_hi, H * W1B + i + 1)
                    nc.gpsimd.tensor_tensor(q2[p][0:D, cols], q_whole[i][0:D], qhi[p][0:D, cols],
                                            ALU.subtract).then_inc(q_ready, 1)

                for p in range(2):
                    for i in range(W1B):
                        q_rest(b * NH + p, p, i)

                def head(H, g, j, left):
                    if left >= 2:
                        pool.wait_ge(q_psum, START + (H + 1) * W1B)
                        stage_wq(H + 2, g, j + 2, j % 2)
                    for t in range(T):
                        n = H * T + t
                        w = weighted_sb[t % 2]
                        pool.wait_ge(weighted, START + n + 1)
                        nc.gpsimd.tensor_tensor(w[:, 0:8, :], w[:, 0:8, :], w[:, 8:16, :], ALU.add).then_inc(tree_step, 1)
                        pool.wait_ge(tree_step, n * 3 + 1)
                        nc.gpsimd.tensor_tensor(w[:, 0:4, :], w[:, 0:4, :], w[:, 4:8, :], ALU.add).then_inc(tree_step, 1)
                        pool.wait_ge(tree_step, n * 3 + 2)
                        nc.gpsimd.tensor_tensor(w[:, 0:2, :], w[:, 0:2, :], w[:, 2:4, :], ALU.add).then_inc(tree_step, 1)
                        pool.wait_ge(tree_step, n * 3 + 3)
                        nc.gpsimd.tensor_tensor(big2[:, t, bass.ds(g * REP * D + j * D, D)], w[:, 0, :], w[:, 1, :],
                                                ALU.add).then_inc(chunks_summed, 1)
                        if t in (HALF + 1, HALF + 3) and left >= 2:
                            q_rest(H + 2, j % 2, (t - HALF) // 2)

                each_head(pool, b, head)

            each_sequence(pool, sequence)

            pool.wait_ge(acc_ready, PLACES * 4 + NT // 4 * E1 * 4)
            chain(pool_step, nc.gpsimd.memset(kst2[D:P, 0:2, :], 0.0), pool, step)
            chain(pool_step, nc.gpsimd.memset(kst2[MROWS, 0:2, :], 1.0), pool, step)
            nc.gpsimd.memset(v1[:, :, :, D:D + 1], 1.0).then_inc(ones_ready, 1)
            with pool.Fori(0, B) as b:
                def stage_qk(H, h, p):
                    pool.nop(nofuse=True)
                    for i, dst in enumerate((wq_dup[p][:], wk_dup[:, p, :])):
                        src = wt[:, bass.ds(col["qkv"] + h * 3 * D + i * D, D)]
                        nc.gpsimd.tensor_copy(dst[:, 0:D], src)
                        last = nc.gpsimd.tensor_copy(dst[:, D:P], src)
                    last.then_inc(w1_ready, 1)

                pool.wait_ge(qk_psum, START + b * NH1 * NP)
                stage_qk(b * NH1, 0, 0)
                stage_qk(b * NH1 + 1, 1, 1)

                def head1(H, h, p, left):
                    if left >= 2:
                        pool.wait_ge(qk_psum, START + (H + 1) * NP)
                        stage_qk(H + 2, h + 2, p)

                each_head1(pool, b, head1)

        @block.scalar
        def _(act):
            for started in (g_ready, mt_ready, mt1_ready):
                act.nop().then_inc(started, START)
            def norm_act(L):
                for b in range(B):
                    act.wait_ge(centered, L * B + b + 1)
                    nc.scalar.activation(sq[:, b * T:(b + 1) * T, :], xn[:, b * T:(b + 1) * T, :],
                                         ACT.Square).then_inc(squared, 1)
                for b in range(B):
                    act.wait_ge(var_ready, L * B + b + 1)
                    nc.scalar.activation(stat[:, 3, b * T:(b + 1) * T], stat[:, 2, b * T:(b + 1) * T],
                                         ACT.Sqrt).then_inc(std_ready, 1)
                for u in range(B * W1B):
                    act.wait_ge(xt_psum, L * B * W1B + u + 1)
                    nc.scalar.copy(xnt[:, u // W1B, bass.ds(1 + u % W1B * BANK, BANK)], ps[:, u % 2, :]).then_inc(xt_copied, 1)

            norm_act(0)
            for u in range(WCOLS // BANK):
                act.wait_ge(w_psum, u + 1)
                nc.scalar.copy(wt[:, u * BANK:(u + 1) * BANK], ps[:, 2 + u % 2, :]).then_inc(w_copied, 1)
            act.wait_ge(dyn_psum, 1)
            act.wait_ge(small_loaded, 16 * 6)
            nc.scalar.activation(sig[:], ps[0:3, 4, 0:B], ACT.Sigmoid, bias=bkgen[:, 0:1]).then_inc(sig_ready, 1)
            act.wait_ge(zeros_ready, 1)

            def copy_keys(b, kv):
                act.wait_ge(k_psum, b * NKV + kv + 1)
                k_ps = ps[:, 2 * (kv % 2):2 * (kv % 2) + 2, :].rearrange("p a b -> p (a b)")
                nc.scalar.copy(kst[:, kv, :], k_ps)
                nc.scalar.copy(kst2[0:D, kv, :], k_ps[0:D]).then_inc(k_hi, 1)

            def copy_values(b, i):
                act.wait_ge(v_psum, b * NV + i + 1)
                v_ps = ps[:, 7, :].rearrange("p (t k d) -> p t k d", t=2, d=D)
                for t in range(2):
                    nc.scalar.copy(vbd[0:D, :, 2 * i + t, 0:D], v_ps[0:D, t])
                    last = nc.scalar.copy(vbd[D:P, :, 2 * i + t, D + 1:OC - 1], v_ps[D:P, t])
                last.then_inc(v_ready, 1)

            for i in range(NKV):
                copy_keys(0, i)
                copy_values(0, i)

            def sequence(b, more):
                def q_leading(H, p, i, bank):
                    act.wait_ge(q_psum, START + H * W1B + i + 1)
                    act.wait_ge(q_ready, W1B + (H - 1) * W1B + i + 1)
                    nc.scalar.mul(q_whole[i][0:D], ps[0:D, bank, :], SCALE)
                    nc.scalar.mul(qhi[p][:, i * BANK:(i + 1) * BANK], ps[:, bank, :], SCALE).then_inc(q_hi, 1)

                def max_rows(H, p, half):
                    act.wait_ge(mt_psum, START + H * 2 + half + 1)
                    for t in range(HALF):
                        c0 = half * BANK + t * P
                        last = nc.scalar.copy(q2[p][MROWS, c0:c0 + P], mt_ps[32 * t:32 * t + 32, :])
                    last.then_inc(mt_ready, 1)

                def exps(H, half, units, tiles_done=None):
                    for blk in units:
                        u = H * 16 + half * 8 + blk
                        act.wait_ge(st_psum, u + 1)
                        if tiles_done is not None:
                            act.wait_ge(pv_psum, START + tiles_done)
                        nc.scalar.activation(big1[:, half, blk, :], ps[:, UNIT_BANK[half][blk], :],
                                             ACT.Exp).then_inc(e_ready, 1)

                def hidden(units):
                    for u in units:
                        f, half = u // W1B, u % W1B
                        act.wait_ge(f1_psum, b * 8 + u + 1)
                        nc.scalar.activation(hmid[:, f, half * BANK:(half + 1) * BANK], ps[:, 4 + u % 2, :], ACT.Relu,
                                             bias=b1e[:, f:f + 1]).then_inc(f1_ready, 1)

                def take_values(g):
                    for t in (0, HALF):
                        nc.scalar.copy(vcur[:, t:t + HALF, :], vbd[:, g, t:t + HALF, :]).then_inc(vcur_ready, 1)

                for i in range(W1B):
                    q_leading(b * NH, 0, i, i)
                act.wait_ge(expert_loaded, b * 64 + 64)
                hidden(range(4))
                for i in range(W1B):
                    q_leading(b * NH + 1, 1, i, i)
                hidden(range(4, 8))
                act.wait_ge(v_ready, (b + 1) * NV)
                take_values(0)
                act.wait_ge(prod_ready, START + b * T)
                for t in range(T):
                    act.wait_ge(f2_psum, b * T + t + 1)
                    nc.scalar.activation(g_cur[:, t, :], ps[:, 2 + t % 2, 0:C], ACT.Silu).then_inc(g_ready, 1)
                max_rows(b * NH, 0, 0)
                exps(b * NH, 0, range(8))

                def head(H, g, j, left):
                    p = j % 2
                    max_rows(H, p, 1)
                    for t in range(T):
                        if t - 1 in QUERY_TILES and left >= 2:
                            q_leading(H + 2, p, QUERY_TILES.index(t - 1), 7)
                        if t < HALF:
                            exps(H, 1, LATE[t], H * T)
                        elif left >= 1:
                            if t == HALF:
                                max_rows(H + 1, 1 - p, 0)
                            exps(H + 1, 0, EARLY[t - HALF], H * T + HALF)
                        if t >= HALF and left == 0 and more:
                            copy_keys(b + 1, t - HALF)
                            copy_values(b + 1, t - HALF)
                    if j == REP - 1 and left >= 1:
                        act.wait_ge(pv_psum, START + H * T + T)
                        take_values(g + 1)

                each_head(act, b, head)
                for t in range(T):
                    act.wait_ge(at_psum, b * T + t + 1)
                    a_ps = ps[:, 2 * (t % 2):2 * (t % 2) + 2, :].rearrange("p a b -> p (a b)")
                    if t >= 2:
                        act.wait_ge(y_psum, b * T + t - 1)
                    nc.scalar.copy(att_t[t % 2][:].rearrange("p a b -> p (a b)"), a_ps).then_inc(at_ready, 1)

            each_sequence(act, sequence)

            norm_act(1)
            for b in range(B):
                act.wait_ge(xt_copied, B * W1B + (b + 1) * W1B)
                nc.scalar.copy(x_hi[:, b * S:(b + 1) * S], xnt[:, b, 1:S + 1]).then_inc(x_hi_ready, 1)
            act.wait_ge(shifted, 1)
            nc.scalar.activation(rt[1], rt[0], ACT.Exp).then_inc(r_exp, 1)
            act.wait_ge(experts_loaded, 16 * 3)
            nc.scalar.copy(up_hi, up_w).then_inc(w_hi_ready, 1)
            nc.scalar.copy(down_hi, down_w).then_inc(w_hi_ready, 1)
            for u in range(NT // 4):
                act.wait_ge(ct_psum, u + 1)
                if u >= 2:
                    act.wait_ge(b2_psum, u - 1)
                nc.scalar.copy(att_t[u % 2][0:E1, 0:4, :].rearrange("p a b -> p (a b)"), ps[0:E1, u % 2, :]).then_inc(ct_ready, 1)
                act.wait_ge(b2_psum, u + 1)
                nc.scalar.copy(gate1[:, 4 * u:4 * u + 4, :].rearrange("p a b -> p (a b)"), ps[:, 2 + u % 2, :]).then_inc(b2_ready, 1)
            with act.Fori(0, NT // 4) as k:
                for e in range(E1):
                    n = k * E1 + e
                    for f in range(F1 // P):
                        act.wait_ge(up_psum, n * 2 + f + 1)
                        if f == 0:
                            act.wait_ge(mid_lo_ready, PLACES + n - 1)
                        nc.scalar.activation(mid1[:, e % 2, f, :], ps[:, 2 * (e % 2) + f, :], ACT.Gelu,
                                             bias=b1_sb[:, f, e:e + 1]).then_inc(up_ready, 1)
                    act.wait_ge(up_ready, n * 2 + 2)
                    act.wait_ge(down_psum, PLACES + n - 1)
                    nc.scalar.copy(mid_hi[:, e % 2], mid1[:, e % 2]).then_inc(mid_hi_ready, 1)
            act.wait_ge(acc_ready, PLACES * 4 + NT // 4 * E1 * 4)
            nc.scalar.activation(gate1, gate1, ACT.Silu).then_inc(gate1_ready, 1)
            with act.Fori(0, B) as b:
                for t in range(T):
                    act.wait_ge(v1_psum, b * T + t + 1)
                    nc.scalar.copy(v1[:, :, t, 0:D], ps[:, 4 + t % 2, :].rearrange("p (h d) -> p h d", d=D)).then_inc(v1_ready, 1)

                def leading(H, p, i):
                    which, half = PARTS[i]
                    cols = slice(half * BANK, (half + 1) * BANK)
                    act.wait_ge(qkf_ready, START + H * NP + i + 1)
                    if which == 0:
                        nc.scalar.mul(qhi[p][:, cols], qkf[0][:, cols], SCALE).then_inc(qk_hi, 1)
                    else:
                        nc.scalar.copy(kst[:, p, cols], qkf[1][:, cols])
                        nc.scalar.copy(kst2[0:D, p, cols], qkf[1][0:D, cols]).then_inc(qk_hi, 1)

                def max_rows1(H, p, half):
                    act.wait_ge(mt1_psum, START + H * 2 + half + 1)
                    for t in range(HALF):
                        c0 = half * BANK + t * P
                        last = nc.scalar.copy(q2[p][MROWS, c0:c0 + P], mt_ps[32 * t:32 * t + 32, :])
                    last.then_inc(mt1_ready, 1)

                def exps1(H, units, tiles_done=None):
                    for half, blk in units:
                        u = H * NU + unit_index(half, blk)
                        act.wait_ge(st_psum1, u + 1)
                        if tiles_done is not None:
                            act.wait_ge(pv1_psum, START + tiles_done)
                        c0 = unit_cols(half, blk)
                        nc.scalar.activation(big1[:, half, blk, c0:BANK], ps[:, unit_bank1(half, blk), c0:BANK],
                                             ACT.Exp).then_inc(e_ready1, 1)

                for p in range(2):
                    for i in range(NP):
                        leading(b * NH1 + p, p, i)
                max_rows1(b * NH1, 0, 0)
                exps1(b * NH1, UNITS[0])

                def head1(H, h, p, left):
                    max_rows1(H, p, 1)
                    for t in range(T):
                        if t < HALF:
                            exps1(H, [UNITS[1][i] for i in LATE[t]], H * T)
                        elif left >= 1:
                            if t == HALF:
                                max_rows1(H + 1, 1 - p, 0)
                            exps1(H + 1, [UNITS[0][i] for i in EARLY1[t - HALF]], H * T + HALF)
                        if t >= HALF and left >= 2:
                            leading(H + 2, p, t - HALF)

                each_head1(act, b, head1)
                for t in range(T):
                    act.wait_ge(at1_psum, b * T + t + 1)
                    if t >= 2:
                        act.wait_ge(y1_psum, b * T + t - 1)
                    nc.scalar.copy(att_t[t % 2][:, 0:4, :].rearrange("p a b -> p (a b)"), ps[:, t % 2, :]).then_inc(at1_ready, 1)

        @block.vector
        def _(dve):
            step = [0]
            for started in (prod_ready, m_ready, weighted, weighted_a, weighted_b, m1_ready, qkf_ready):
                dve.nop().then_inc(started, START)
            dve.nop().then_inc(att1_ready, PLACES)
            dve.nop().then_inc(mid_lo_ready, PLACES)
            dve.nop().then_inc(acc_ready, PLACES * 4)
            dve.nop().then_inc(qk_ready, NP)

            def do(ins):
                chain(dve_step, ins, dve, step)

            dve.wait_ge(ident_ready, 1)
            do(nc.vector.tensor_copy(ident_h[:], ident[:]))
            do(nc.vector.tensor_reduce(row_chunk[:], ident[:].rearrange("p (s c) -> p c s", c=16), AX, ALU.add))
            nc.vector.tensor_copy(ident_f16[:], ident[:])
            dve.wait_ge(zeros_ready, 1)
            for kv in range(NKV):
                last = nc.vector.tensor_copy(kst2[MROWS, kv, :].rearrange("p (c k) -> p c k", k=D),
                                             wide(row_chunk[MROWS, :], D))
            last.then_inc(spread_ready, 1)
            do(nc.vector.memset(ps[:, 6, 2 * OC:3 * OC], 0.0))
            do(nc.vector.memset(o_ps[:, 2, 4:6, D:D + 1], 1.0))

            def norm_dve(L):
                bs = lambda b: slice(b * T, (b + 1) * T)
                for b in range(B):
                    if L == 0:
                        dve.wait_ge(x_loaded[b], 16)
                    do(nc.vector.tensor_reduce(stat[:, 0, bs(b)], x_sb[:, bs(b), :], AX, ALU.add))
                    do(nc.vector.tensor_scalar(stat[:, 1, bs(b)], stat[:, 0, bs(b)], 1.0 / C, None, ALU.mult))
                    nc.vector.tensor_tensor(xn[:, bs(b), :], x_sb[:, bs(b), :], wide(stat[:, 1, bs(b)], C),
                                            ALU.subtract).then_inc(centered, 1)
                for b in range(B):
                    dve.wait_ge(squared, L * B + b + 1)
                    do(nc.vector.tensor_reduce(stat[:, 0, bs(b)], sq[:, bs(b), :], AX, ALU.add))
                    nc.vector.tensor_scalar(stat[:, 2, bs(b)], stat[:, 0, bs(b)], 1.0 / C, EPS, ALU.mult,
                                            ALU.add).then_inc(var_ready, 1)
                for b in range(B):
                    dve.wait_ge(std_ready, L * B + b + 1)
                    do(nc.vector.reciprocal(stat[:, 0, bs(b)], stat[:, 3, bs(b)]))
                    dve.wait_ge(centered, L * B + b + 1)
                    nc.vector.tensor_tensor(xn[:, bs(b), :], xn[:, bs(b), :], wide(stat[:, 0, bs(b)], C),
                                            ALU.mult).then_inc(normed, 1)

            norm_dve(0)
            for b in range(B):
                dve.wait_ge(xt_copied, W1B * (b + 1))
                do(nc.vector.tensor_reduce(stat[:, 1, b:b + 1], xnt[:, b, 1:S + 1], AX, ALU.add))
            nc.vector.tensor_scalar(ctx_mean[:], stat[:, 1, 0:B], 1.0 / S, None, ALU.mult).then_inc(ctx_ready, 1)
            dve.wait_ge(route_psum, 1)
            for b in range(B):
                do(nc.vector.tensor_tensor(route[:, b, :], ps[0:1, 5, b * E0:(b + 1) * E0], br0_sb[:], ALU.add))
                do(nc.vector.max(route_max[:, b, :], route[:, b, :]))
                last = nc.vector.max_index(route_idx[:, b, :], route_max[:, b, :], route[:, b, :])
                if b < B - 1:
                    do(last)
            last.then_inc(route_ready, 1)
            dve.wait_ge(gate_psum, 1)
            do(nc.vector.tensor_copy(gate[:], ps[:, 4, 8:8 + B]))
            for b in range(B):
                do(nc.vector.tensor_scalar(conv_wg[:, b, 0:3], conv_w[:], gate[:, b:b + 1], None, ALU.mult))
                do(nc.vector.tensor_tensor(conv_wg[:, b, 3:4], conv_b[:], gate[:, b:b + 1], ALU.mult))

            def convolve(b, k):
                wg = lambda k: conv_wg[:, b, k:k + 1]
                if k == 0:
                    nc.vector.tensor_scalar(hcur[:], xnt[:, b, 1:S + 1], wg(1), wg(3), ALU.mult,
                                            ALU.add).then_inc(conv_step, 1)
                else:
                    dve.wait_ge(conv_step, b * 2 + k)
                    first = 0 if k == 1 else 2
                    nc.vector.scalar_tensor_tensor(out=hcur[:], in0=xnt[:, b, first:first + S], scalar=wg(first),
                                                   in1=hcur[:], op0=ALU.mult,
                                                   op1=ALU.add).then_inc(conv_step if k == 1 else conv_ready, 1)

            def keys_rest(b, kv):
                dve.wait_ge(k_hi, b * NKV + kv + 1)
                k_ps = ps[:, 2 * (kv % 2):2 * (kv % 2) + 2, :].rearrange("p a b -> p (a b)")
                nc.vector.tensor_tensor(kst[D:P, kv, :], k_ps[D:P], kst[D:P, kv, :], ALU.subtract).then_inc(k_ready, 1)

            for k in range(3):
                convolve(0, k)
            for kv in range(NKV):
                keys_rest(0, kv)

            def sequence(b, more):
                def maxima(H, t, bank=0):
                    dve.wait_ge(s_psum, H * T + t + 1)
                    if t % HALF == 0:
                        dve.wait_ge(m_ready, START + H * 2 + t // HALF)
                    nc.vector.tensor_reduce(negm[:, t % HALF, :],
                                            ps[:, bank:bank + 2, :].rearrange("p a (c k) -> p (a c) k", k=D), AX,
                                            ALU.max, negate=True).then_inc(s_max, 1)
                    if t % HALF == HALF - 1:
                        n = H * 2 + t // HALF
                        dve.wait_ge(s_max, H * T + t + 1)
                        dve.wait_ge(mt_psum, START + n)
                        nc.vector.tensor_scalar(mhl[:, :, 0:16], negm[:], F16_MAX, -F16_MAX, ALU.min,
                                                ALU.max).then_inc(mhi_ready, 1)
                        dve.wait_ge(mhi_ready, n + 1)
                        nc.vector.tensor_tensor(mhl[:, :, 16:32], negm[:], mhl[:, :, 0:16], ALU.subtract).then_inc(m_ready, 1)

                for t in range(T):
                    maxima(b * NH, t, 4 * (t % 2))

                def head(H, g, j, left):
                    for t in range(T):
                        n = H * T + t
                        w, sw = weighted_sb[t % 2], sumw[j % 2]
                        z = o_ps[:, :, :, D]
                        dve.wait_ge(pv_psum, START + n + 1)
                        nc.vector.reciprocal(places(zinv[:]), z).then_inc(inv_ready, 1)
                        dve.wait_ge(inv_ready, n + 1)
                        nc.vector.tensor_tensor(places(sw[:, t, :]), z, places(zinv[:]), ALU.mult).then_inc(sumw_ready, 1)
                        dve.wait_ge(sumw_ready, n + 1)
                        nc.vector.tensor_tensor(coef[:], sw[:, t, :], zinv[:], ALU.mult).then_inc(coef_ready, 1)
                        dve.wait_ge(coef_ready, n + 1)
                        dve.wait_ge(chunks_summed, n + 1)
                        nc.vector.tensor_tensor(w[:, 12:16, :], o_ps[:, 2, 0:4, 0:D], wide(coef[:, 12:16], D),
                                                ALU.mult).then_inc(weighted_a, 1)
                        nc.vector.tensor_tensor(w[:, 0:6, :], o_ps[:, 0, :, 0:D], wide(coef[:, 0:6], D),
                                                ALU.mult).then_inc(weighted_b, 1)
                        nc.vector.tensor_tensor(w[:, 6:12, :], o_ps[:, 1, :, 0:D], wide(coef[:, 6:12], D),
                                                ALU.mult).then_inc(weighted, 1)
                        if left >= 1:
                            maxima(H + 1, t)
                        if left == 0 and more:
                            if t == 0:
                                dve.wait_ge(q_psum, START + (H + 1) * W1B)
                            if t < 3:
                                convolve(b + 1, t)
                            if t >= HALF:
                                keys_rest(b + 1, t - HALF)
                    nc.vector.tensor_reduce(total[:, bass.ds(g * REP + j, 1), :].rearrange("p a t -> p (a t)"),
                                            sw[:, :, 0:NCH], AX, ALU.add).then_inc(total_ready, 1)

                each_head(dve, b, head)
                dve.wait_ge(total_ready, (b + 1) * NH)
                nc.vector.tensor_scalar(tinv[:], total[:], 1e-9, None, ALU.add).then_inc(tinv_ready, 1)
                dve.wait_ge(tinv_ready, b * 2 + 1)
                nc.vector.reciprocal(tinv[:], tinv[:]).then_inc(tinv_ready, 1)
                dve.wait_ge(tinv_ready, b * 2 + 2)
                dve.wait_ge(chunks_summed, (b + 1) * NH * T + 2)
                for t in range(T):
                    heads = big2[:, t, :].rearrange("p (h d) -> p h d", d=D)
                    nc.vector.tensor_tensor(heads, heads, wide(tinv[:, :, t], D), ALU.mult).then_inc(att_normed, 1)
                dve.wait_ge(g_ready, START + ((b + 1) * T))
                for t in range(T):
                    dve.wait_ge(y_psum, b * T + t + 1)
                    nc.vector.tensor_tensor(prod[t % 2][:], ps[:, 4 + t % 2, 0:C], g_cur[:, t, :], ALU.mult).then_inc(prod_ready, 1)
                    dve.wait_ge(prod_ready, START + b * T + t + 1)
                    xt = x_sb[:, bass.ds(b * T + t, 1), :].rearrange("p a c -> p (a c)")
                    nc.vector.tensor_tensor(xt, xt, prod[t % 2][:], ALU.add).then_inc(x_ready, 1)

            each_sequence(dve, sequence)

            dve.wait_ge(x_ready, B * T)
            norm_dve(1)
            do(nc.vector.memset(mhl[:], 0.0))
            for b in range(B):
                dve.wait_ge(x_hi_ready, b + 1)
                nc.vector.tensor_tensor(x_lo[:, b * S:(b + 1) * S], xnt[:, b, 1:S + 1], x_hi[:, b * S:(b + 1) * S],
                                        ALU.subtract).then_inc(x_lo_ready, 1)
            dve.wait_ge(logits_psum, 1)
            dve.wait_ge(pos_loaded, 16 * 7)
            logits = ps[:, 6, :].rearrange("p (t e) -> p t e", e=E1)
            rb = br1_sb[:].unsqueeze(1).to_broadcast([P, NT, E1])
            row = stat[:, 0, :]
            do(nc.vector.tensor_tensor(rt[0], logits, rb, ALU.add))
            do(nc.vector.tensor_reduce(row, rt[0], AX, ALU.max))
            nc.vector.tensor_tensor(rt[0], rt[0], wide(row, E1), ALU.subtract).then_inc(shifted, 1)
            dve.wait_ge(r_exp, 1)
            do(nc.vector.tensor_reduce(stat[:, 1, :], rt[1], AX, ALU.add))
            do(nc.vector.reciprocal(stat[:, 2, :], stat[:, 1, :]))
            do(nc.vector.tensor_tensor(rt[2], rt[1], wide(stat[:, 2, :], E1), ALU.mult))
            for t in range(NT):
                last = nc.vector.max(top8[:, t, :], rt[2][:, t, :])
            do(last)
            fourth = top8[:, :, 3:4].to_broadcast([P, NT, E1])
            dve.wait_ge(masks_ready, 1)
            do(nc.vector.tensor_tensor(rt[3], rt[2], fourth, ALU.is_gt))
            do(nc.vector.tensor_tensor(rt[4], rt[2], fourth, ALU.is_equal))
            do(nc.vector.tensor_reduce(stat[:, 3, :], rt[3], AX, ALU.add))
            one_dim = lambda ap: ap.rearrange("p t e -> p (t e)")
            do(nc.vector.tensor_tensor_scan(one_dim(rt[5]), one_dim(carry[:]), one_dim(rt[4]), 0.0, ALU.mult, ALU.add))
            do(nc.vector.tensor_tensor(rt[5], rt[5], wide(stat[:, 3, :], E1), ALU.add))
            do(nc.vector.tensor_scalar(rt[6], rt[5], 4.0, None, ALU.is_le))
            do(nc.vector.tensor_tensor(rt[4], rt[4], rt[6], ALU.mult))
            do(nc.vector.tensor_tensor(rt[3], rt[3], rt[4], ALU.add))
            do(nc.vector.tensor_tensor(rt[2], rt[2], rt[3], ALU.mult))
            do(nc.vector.tensor_reduce(stat[:, 1, :], rt[2], AX, ALU.add))
            do(nc.vector.reciprocal(stat[:, 2, :], stat[:, 1, :]))
            nc.vector.tensor_tensor(share[:], rt[2], wide(stat[:, 2, :], E1), ALU.mult).then_inc(share_ready, 1)
            for i, (table, whole, leading) in enumerate(((UP_LO, up_w, up_hi),
                                                         (DOWN_LO, down_w.rearrange("p e f c -> p e (f c)"),
                                                          down_hi.rearrange("p e f c -> p e (f c)")))):
                dve.wait_ge(w_hi_ready, i + 1)
                for place, first, count in table:
                    nc.vector.tensor_tensor(place.rearrange("p (e f) -> p e f", e=count), whole[:, first:first + count, :],
                                            leading[:, first:first + count, :], ALU.subtract).then_inc(w_lo_ready, 1)
            dve.wait_ge(share_ready, 1)

            def split_middle(n, place):
                dve.wait_ge(mid_hi_ready, n + 1)
                nc.vector.tensor_tensor(mid_lo[:, place], mid1[:, place], mid_hi[:, place],
                                        ALU.subtract).then_inc(mid_lo_ready, 1)

            def chunk(k, more):
                for e in range(E1):
                    if more or e < E1 - 1:
                        split_middle(k * E1 + e + 1, (e + 1) % 2)
                    dve.wait_ge(down_psum, PLACES + k * E1 + e + 1)
                    for t in range(4):
                        n = k * E1 * 4 + e * 4 + t
                        whole = gate1[:, bass.ds(k * 4 + t, 1), :].rearrange("p a c -> p (a c)")
                        src = whole if e == 0 else acc[:, t, :]
                        dst = whole if e == E1 - 1 else acc[:, t, :]
                        dve.wait_ge(acc_ready, PLACES * 4 + n - 3)
                        nc.vector.scalar_tensor_tensor(
                            out=dst, in0=ps[:, 4 + e % 2, t * C:(t + 1) * C],
                            scalar=share[:, bass.ds(k * 4 + t, 1), e:e + 1].rearrange("p a c -> p (a c)"), in1=src,
                            op0=ALU.mult, op1=ALU.add).then_inc(acc_ready, 1)

            split_middle(0, 0)
            dve.wait_ge(b2_ready, NT // 4)
            with dve.Fori(0, NT // 4 - 1) as k:
                chunk(k, True)
            chunk(NT // 4 - 1, False)

            with dve.Fori(0, B) as b:
                nc.vector.tensor_copy(hcur[:], xnt[:, b, 1:S + 1]).then_inc(h1_ready, 1)

                def add_positions(H, i):
                    which, half = PARTS[i]
                    cols = slice(half * BANK, (half + 1) * BANK)
                    dve.wait_ge(qk_psum, START + H * NP + i + 1)
                    dve.wait_ge(qk_ready, NP + H * NP + i - NP + 1)
                    nc.vector.tensor_tensor(qkf[which][:, cols], ps[:, 6, :], pos2[:, cols],
                                            ALU.add).then_inc(qkf_ready, 1)

                def rest(H, p, i):
                    which, half = PARTS[i]
                    cols = slice(half * BANK, (half + 1) * BANK)
                    dve.wait_ge(qk_hi, H * NP + i + 1)
                    if which == 0:
                        nc.vector.scalar_tensor_tensor(out=q2[p][0:D, cols], in0=qkf[0][0:D, cols], scalar=SCALE,
                                                       in1=qhi[p][0:D, cols], op0=ALU.mult,
                                                       op1=ALU.subtract).then_inc(qk_ready, 1)
                    else:
                        nc.vector.tensor_tensor(kst[D:P, p, cols], qkf[1][D:P, cols], kst[D:P, p, cols],
                                                ALU.subtract).then_inc(qk_ready, 1)

                def maxima1(H, t):
                    dve.wait_ge(s1_psum, H * T + t + 1)
                    if t % HALF == 0:
                        dve.wait_ge(m1_ready, START + H * 2 + t // HALF)
                    nc.vector.tensor_reduce(negm1[:, t % HALF, :], s_ps[:, 0:(t + 1) * P], AX, ALU.max,
                                            negate=True).then_inc(s1_max, 1)
                    if t % HALF == HALF - 1:
                        n = H * 2 + t // HALF
                        dve.wait_ge(s1_max, H * T + t + 1)
                        dve.wait_ge(mt1_psum, START + n)
                        nc.vector.tensor_scalar(mhl[:, :, 0:1], negm1[:], F16_MAX, -F16_MAX, ALU.min,
                                                ALU.max).then_inc(mhi1_ready, 1)
                        dve.wait_ge(mhi1_ready, n + 1)
                        nc.vector.tensor_tensor(mhl[:, :, 16:17], negm1[:], mhl[:, :, 0:1],
                                                ALU.subtract).then_inc(m1_ready, 1)

                for i in range(NP + 1):
                    if i < NP:
                        add_positions(b * NH1, i)
                    if i > 0:
                        rest(b * NH1, 0, i - 1)
                for t in range(T):
                    maxima1(b * NH1, t)
                    if t < NP:
                        add_positions(b * NH1 + 1, t)
                    if 1 <= t <= NP:
                        rest(b * NH1 + 1, 1, t - 1)

                def head1(H, h, p, left):
                    for t in range(T):
                        n = H * T + t
                        dve.wait_ge(pv1_psum, START + n + 1)
                        nc.vector.reciprocal(zinv1[:, t:t + 1], ps[:, 4 + t % 2, D:D + 1]).then_inc(inv1_ready, 1)
                        if t - 1 in PART_TILES and left >= 2:
                            add_positions(H + 2, PART_TILES.index(t - 1))
                        if left >= 1:
                            maxima1(H + 1, t)
                        dve.wait_ge(inv1_ready, n + 1)
                        nc.vector.tensor_scalar(att1[:, t, bass.ds(h * D, D)], ps[:, 4 + t % 2, 0:D], zinv1[:, t:t + 1],
                                                None, ALU.mult).then_inc(att1_ready, 1)
                        if left >= 2:
                            if t >= HALF:
                                rest(H + 2, p, t - HALF)

                each_head1(dve, b, head1)
                dve.wait_ge(gate1_ready, 1)
                for t in range(T):
                    dve.wait_ge(y1_psum, b * T + t + 1)
                    gt = gate1[:, bass.ds(b * T + t, 1), :].rearrange("p a c -> p (a c)")
                    nc.vector.tensor_tensor(prod[t % 2][:], ps[:, 4 + t % 2, 0:C], gt, ALU.mult).then_inc(prod1_ready, 1)
                    dve.wait_ge(prod1_ready, b * T + t + 1)
                    xt = x_sb[:, bass.ds(b * T + t, 1), :].rearrange("p a c -> p (a c)")
                    nc.vector.tensor_tensor(xt, xt, prod[t % 2][:], ALU.add).then_inc(x1_ready, 1)

        @block.tensor
        def _(pe):
            pe.nop().then_inc(down_psum, PLACES)
            for started in (q_psum, pv_psum, mt_psum, qk_psum, mt1_psum, pv1_psum):
                pe.nop().then_inc(started, START)
            def norm_pe(L):
                for u in range(B * W1B):
                    pe.wait_ge(normed, L * B + u // W1B + 1)
                    if u >= 2:
                        pe.wait_ge(xt_copied, L * B * W1B + u - 1)
                    for i in range(4):
                        last = nc.tensor.transpose(ps[:, u % 2, i * P:(i + 1) * P], xn[:, u * 4 + i, :], ident[:])
                    last.then_inc(xt_psum, 1)

            pe.wait_ge(ident_ready, 1)
            norm_pe(0)
            pe.wait_ge(weights_loaded, 16 * len(names))
            for u in range(WCOLS // BANK):
                if u >= 2:
                    pe.wait_ge(w_copied, u - 1)
                for i in range(4):
                    k = (u * 4 + i) * P
                    last = nc.tensor.transpose(ps[:, 2 + u % 2, i * P:(i + 1) * P], wraw[:, k:k + P], ident[:])
                last.then_inc(w_psum, 1)
            pe.wait_ge(ctx_ready, 1)
            pe.wait_ge(small_loaded, 16 * 6)
            pe.wait_ge(consts_ready, 1)
            nc.tensor.matmul(ps[0:3, 4, 0:B], kgen_t[:], ctx_mean[:], start=True, stop=True).then_inc(dyn_psum, 1)
            for b in range(B):
                last = nc.tensor.matmul(ps[0:1, 5, b * E0:(b + 1) * E0], ctx_mean[:, b:b + 1], wr0_sb[:],
                                        start=True, stop=True)
            last.then_inc(route_psum, 1)
            pe.wait_ge(sig_ready, 1)
            nc.tensor.matmul(ps[:, 4, 8:8 + B], third[:], sig[:], start=True, stop=True).then_inc(gate_psum, 1)
            pe.wait_ge(wk_ready, 1)
            pe.wait_ge(spread_ready, 1)
            pe.wait_ge(xt_copied, B * W1B)
            pe.wait_ge(w_copied, WCOLS // BANK)
            pe.wait_ge(conv_ready, 1)
            pe.wait_ge(zeros_ready, 1)

            def project_keys(b, kv):
                if kv >= 2:
                    pe.wait_ge(k_ready, b * NKV + kv - 1)
                for i in range(W1B):
                    last = nc.tensor.matmul(ps[:, 2 * (kv % 2) + i, :], wk_dup[:, kv, :],
                                            hcur[:, i * BANK:(i + 1) * BANK], start=True, stop=True)
                last.then_inc(k_psum, 1)

            def project_values(b, i):
                if i >= 1:
                    pe.wait_ge(v_ready, b * NV + i)
                for t in range(2):
                    last = nc.tensor.matmul(ps[:, 7, t * NKV * D:(t + 1) * NKV * D],
                                            hcur[:, (2 * i + t) * P:(2 * i + t + 1) * P],
                                            wt[:, col["v"]:col["v"] + NKV * D], start=True, stop=True)
                last.then_inc(v_psum, 1)

            project_keys(0, 0)
            for i in range(NV):
                if i + 1 < NKV:
                    project_keys(0, i + 1)
                project_values(0, i)

            def sequence(b, more):
                def hidden(units):
                    for u in units:
                        f, half = u // W1B, u % W1B
                        if u >= 2:
                            pe.wait_ge(f1_ready, b * 8 + u - 1)
                        nc.tensor.matmul(ps[:, 4 + u % 2, :], w1e[:, f * P:(f + 1) * P],
                                         xnt[:, b, bass.ds(1 + half * BANK, BANK)], start=True,
                                         stop=True).then_inc(f1_psum, 1)

                def gate_tile(t):
                    if t >= 2:
                        pe.wait_ge(g_ready, START + b * T + t - 1)
                    for f in range(F0 // P):
                        nc.tensor.matmul(ps[:, 2 + t % 2, 0:C], hmid[:, f, t * P:(t + 1) * P], w2e[:, f, :],
                                         start=(f == 0), stop=False)
                    nc.tensor.matmul(ps[:, 2 + t % 2, 0:C], ones_row[:], b2e[:], start=False,
                                     stop=True).then_inc(f2_psum, 1)

                def queries(H, p, i, bank):
                    if i == 0:
                        pe.wait_ge(wq_ready, H + 1)
                    nc.tensor.matmul(ps[:, bank, :], wq_dup[p][:], hcur[:, i * BANK:(i + 1) * BANK],
                                     start=True, stop=True).then_inc(q_psum, 1)

                def scores(H, g, p, t, bank=0):
                    for i in range(W1B):
                        last = nc.tensor.matmul(ps[:, bank + i, :], qhi[p][:, t * P:(t + 1) * P],
                                                kst[:, g, i * BANK:(i + 1) * BANK], start=True, stop=True)
                    last.then_inc(s_psum, 1)

                def turn_maxima(H, half):
                    pe.wait_ge(m_ready, START + H * 2 + half + 1)
                    nc.tensor.transpose(mt_ps, mhl[:].rearrange("p a b -> p (a b)"), ident_f16[:]).then_inc(mt_psum, 1)

                def turned_scores(H, g, p, half, units):
                    for blk in units:
                        u = H * 16 + half * 8 + blk
                        if blk == units[0]:
                            pe.wait_ge(mt_ready, START + H * 2 + half + 1)
                        if UNIT_BEFORE[half][blk] is not None:
                            pe.wait_ge(e_ready, u - blk + UNIT_BEFORE[half][blk] + 1)
                        dst = ps[:, UNIT_BANK[half][blk], :]
                        kb = kst[:, g, blk * P:(blk + 1) * P]
                        nc.tensor.matmul(dst, kb, qhi[p][:, half * BANK:(half + 1) * BANK], start=True, stop=False)
                        nc.tensor.matmul(dst, kst2[:, g, blk * P:(blk + 1) * P], q2[p][:, half * BANK:(half + 1) * BANK],
                                         start=False, stop=True).then_inc(st_psum, 1)

                pe.wait_ge(k_ready, (b + 1) * NKV)
                pe.wait_ge(v_ready, (b + 1) * NV)
                for i in range(W1B):
                    queries(b * NH, 0, i, i)
                pe.wait_ge(expert_loaded, b * 64 + 64)
                pe.wait_ge(prod_ready, START + b * T)
                hidden(range(4))
                for i in range(W1B):
                    pe.wait_ge(q_hi, b * NH * W1B + i + 1)
                    queries(b * NH + 1, 1, i, i)
                hidden(range(4, 8))
                pe.wait_ge(q_hi, (b * NH + 2) * W1B)
                pe.wait_ge(f1_ready, b * 8 + 8)
                for t in range(T):
                    if t >= 2:
                        pe.wait_ge(s_max, b * NH * T + t - 1)
                    scores(b * NH, 0, 0, t, 4 * (t % 2))
                    if t < HALF:
                        gate_tile(2 * t)
                        gate_tile(2 * t + 1)
                    if t == HALF:
                        turn_maxima(b * NH, 0)
                        pe.wait_ge(g_ready, START + (b + 1) * T)
                        pe.wait_ge(q_ready, W1B + (b * NH + 1) * W1B)
                    if t >= HALF:
                        turned_scores(b * NH, 0, 0, 0, (2 * t - 8, 2 * t - 7))
                pe.wait_ge(s_max, b * NH * T + T)
                pe.nop(nofuse=True)

                def head(H, g, j, left):
                    p = j % 2
                    g_next, p_next = (g, 1 - p) if j < REP - 1 else (g + 1, 1 - p)
                    for t in range(T):
                        n = H * T + t
                        for blk in range(T):
                            if blk == 0:
                                pe.wait_ge(weighted_a, START + n)
                            if blk == 2:
                                pe.wait_ge(weighted_b, START + n)
                            if blk == 5:
                                pe.wait_ge(weighted, START + n)
                            if j == 0 and t == 0 and blk % HALF == 0:
                                pe.wait_ge(vcur_ready, (b * NKV + g) * 2 + blk // HALF + 1)
                            if t % HALF == 0:
                                pe.wait_ge(e_ready, H * 16 + t // HALF * 8 + blk + 1)
                            bank, place = product_place(blk)
                            last = nc.tensor.matmul(ps[:, bank, bass.ds(place * OC, OC)],
                                                    big1[:, t // HALF, blk, bass.ds(t % HALF * P, P)],
                                                    vcur[:, blk, :], start=True, stop=True)
                        last.then_inc(pv_psum, 1)
                        if left >= 1:
                            pe.wait_ge(s_max, (H + 1) * T + t)
                            scores(H + 1, g_next, p_next, t)
                        if t == 0:
                            turn_maxima(H, 1)
                        if t == HALF and left >= 1:
                            if left >= 2:
                                pe.wait_ge(q_hi, (H + 2) * W1B + 1)
                            turn_maxima(H + 1, 0)
                        if t < HALF:
                            turned_scores(H, g, p, 1, LATE[t])
                        elif left >= 1:
                            turned_scores(H + 1, g_next, p_next, 0, EARLY[t - HALF])
                        if left == 0 and more and t >= HALF - 1:
                            kv = t - HALF + 1
                            if kv == 0:
                                pe.wait_ge(conv_ready, b + 2)
                                pe.wait_ge(s_max, (b + 1) * NH * T)
                            if kv == 1:
                                pe.wait_ge(mt_ready, START + (b + 1) * NH * 2)
                                pe.wait_ge(e_ready, (b + 1) * NH * 16)
                            if kv < NKV:
                                project_keys(b + 1, kv)
                            if kv >= 1:
                                project_values(b + 1, kv - 1)
                        if t in QUERY_TILES and left >= 2:
                            if t < HALF:
                                pe.wait_ge(e_ready, H * 16 + 8 + 6)
                            queries(H + 2, p, QUERY_TILES.index(t), 7)

                each_head(pe, b, head)

                def turn_output(t):
                    pe.wait_ge(att_normed, b * T + t + 1)
                    if t >= 2:
                        pe.wait_ge(at_ready, b * T + t - 1)
                    for f in range(8):
                        last = nc.tensor.transpose(ps[:, 2 * (t % 2) + f // 4, bass.ds(f % 4 * P, P)],
                                                   big2[:, t, f * P:(f + 1) * P], ident[:])
                    last.then_inc(at_psum, 1)

                turn_output(0)
                for t in range(T):
                    if t + 1 < T:
                        turn_output(t + 1)
                    if t >= 2:
                        pe.wait_ge(prod_ready, START + b * T + t - 1)
                    pe.wait_ge(at_ready, b * T + t + 1)
                    for f in range(8):
                        last = nc.tensor.matmul(ps[:, 4 + t % 2, 0:C], att_t[t % 2][:, f, :],
                                                wt[:, col["o"] + f * P:col["o"] + (f + 1) * P],
                                                start=(f == 0), stop=(f == 7))
                    last.then_inc(y_psum, 1)

            each_sequence(pe, sequence)

            norm_pe(1)
            pe.wait_ge(xt_copied, 2 * B * W1B)
            pe.wait_ge(pos_loaded, 16 * 7)
            tile = lambda n: xnt[:, n // T, 1 + n % T * P:1 + (n % T + 1) * P]
            for n in range(NT):
                last = nc.tensor.matmul(ps[:, 6, n * E1:(n + 1) * E1], tile(n), wr1_sb[:], start=True, stop=True)
            last.then_inc(logits_psum, 1)
            pe.wait_ge(share_ready, 1)

            def turn_shares(u):
                if u >= 2:
                    pe.wait_ge(ct_ready, u - 1)
                for i in range(4):
                    last = nc.tensor.transpose(ps[0:E1, u % 2, i * P:(i + 1) * P], share[:, 4 * u + i, :], ident[:])
                last.then_inc(ct_psum, 1)

            turn_shares(0)
            for u in range(NT // 4):
                if u + 1 < NT // 4:
                    turn_shares(u + 1)
                pe.wait_ge(ct_ready, u + 1)
                if u >= 2:
                    pe.wait_ge(b2_ready, u - 1)
                for i in range(4):
                    last = nc.tensor.matmul(ps[:, 2 + u % 2, i * P:(i + 1) * P], att_t[u % 2][0:E1, i, :], b2_sb[:],
                                            start=True, stop=True)
                last.then_inc(b2_psum, 1)
            pe.wait_ge(b2_ready, NT // 4)
            pe.wait_ge(x_lo_ready, B)
            pe.wait_ge(w_lo_ready, len(UP_LO) + len(DOWN_LO))

            def up(k, e, wait=True):
                for f in range(F1 // P):
                    if wait:
                        pe.wait_ge(up_ready, (k * E1 + e) * 2 + f - 3)
                    dst = ps[:, 2 * (e % 2) + f, :]
                    tokens = bass.ds(k * BANK, BANK)
                    hi, lo = up_hi[:, e, f * P:(f + 1) * P], lesser(UP_LO, e)[:, f * P:(f + 1) * P]
                    nc.tensor.matmul(dst, hi, x_hi[:, tokens], start=True, stop=False)
                    nc.tensor.matmul(dst, hi, x_lo[:, tokens], start=False, stop=False)
                    nc.tensor.matmul(dst, lo, x_hi[:, tokens], start=False, stop=True).then_inc(up_psum, 1)

            def down(k, e):
                n = k * E1 + e
                pe.wait_ge(mid_lo_ready, PLACES + n + 1)
                pe.wait_ge(acc_ready, (PLACES + n - 1) * 4)
                for t in range(4):
                    dst = ps[:, 4 + e % 2, t * C:(t + 1) * C]
                    for f in range(F1 // P):
                        hi, lo = mid_hi[:, e % 2, f, t * P:(t + 1) * P], mid_lo[:, e % 2, f, t * P:(t + 1) * P]
                        w_hi, w_lo = down_hi[:, e, f, :], lesser(DOWN_LO, e)[:, f * C:(f + 1) * C]
                        nc.tensor.matmul(dst, hi, w_hi, start=(f == 0), stop=False)
                        nc.tensor.matmul(dst, hi, w_lo, start=False, stop=False)
                        last = nc.tensor.matmul(dst, lo, w_hi, start=False, stop=(f == F1 // P - 1))
                last.then_inc(down_psum, 1)

            def chunk(k, more):
                for e in range(E1):
                    if e + 2 < E1:
                        up(k, e + 2)
                    elif more:
                        up(k + 1, e + 2 - E1)
                    down(k, e)

            up(0, 0, wait=False)
            up(0, 1, wait=False)
            with pe.Fori(0, NT // 4 - 1) as k:
                chunk(k, True)
            chunk(NT // 4 - 1, False)

            pe.wait_ge(ones_ready, 1)
            pe.wait_ge(acc_ready, PLACES * 4 + NT // 4 * E1 * 4)
            with pe.Fori(0, B) as b:
                pe.wait_ge(h1_ready, b + 1)
                for t in range(T):
                    if t >= 2:
                        pe.wait_ge(v1_ready, b * T + t - 1)
                    wv = wt[:, col["qkv"]:col["qkv"] + NH1 * 3 * D].rearrange("p (h d) -> p h d", h=NH1)
                    nc.tensor.matmul(ps[:, 4 + t % 2, :], hcur[:, t * P:(t + 1) * P], wv[:, :, 2 * D:3 * D],
                                     start=True, stop=True).then_inc(v1_psum, 1)

                def project(H, p, i):
                    which, half = PARTS[i]
                    if i == 0:
                        pe.wait_ge(w1_ready, H + 1)
                    pe.wait_ge(qkf_ready, START + H * NP + i)
                    nc.tensor.matmul(ps[:, 6, :], wq_dup[p][:] if which == 0 else wk_dup[:, p, :],
                                     hcur[:, half * BANK:(half + 1) * BANK], start=True, stop=True).then_inc(qk_psum, 1)

                def scores1(H, p, t, wait):
                    if wait:
                        pe.wait_ge(s1_max, H * T + t)
                    last_bank = t * P // BANK
                    for c in range(last_bank + 1):
                        n = min(BANK, (t + 1) * P - c * BANK)
                        last = nc.tensor.matmul(ps[:, c, 0:n], qhi[p][:, t * P:(t + 1) * P],
                                                kst[:, p, c * BANK:c * BANK + n], start=True, stop=(c < last_bank))
                    d = t * P % BANK
                    nc.tensor.matmul(ps[:, last_bank, d:d + P], ident_h[:], mask_qk[:], start=False,
                                     stop=True).then_inc(s1_psum, 1)

                def turn_maxima1(H, half, first=False):
                    pe.wait_ge(m1_ready, START + H * 2 + half + 1)
                    if not first:
                        pe.wait_ge(e_ready1, H * NU + half * HALF)
                    nc.tensor.transpose(mt_ps, mhl[:].rearrange("p a b -> p (a b)"), ident_f16[:]).then_inc(mt1_psum, 1)

                def turned_scores1(H, p, units, first=False):
                    for half, blk in units:
                        u = H * NU + unit_index(half, blk)
                        c0 = unit_cols(half, blk)
                        if blk == 0 or (half, blk) == units[0]:
                            pe.wait_ge(mt1_ready, START + H * 2 + half + 1)
                        if not (first and blk < 3):
                            pe.wait_ge(e_ready1, u - 2)
                        dst = ps[:, unit_bank1(half, blk), c0:BANK]
                        kb = kst[:, p, blk * P:(blk + 1) * P]
                        q0 = half * BANK + c0
                        nc.tensor.matmul(dst, kb, qhi[p][:, q0:(half + 1) * BANK], start=True, stop=False)
                        last = nc.tensor.matmul(dst, kst2[:, p, blk * P:(blk + 1) * P], q2[p][:, q0:(half + 1) * BANK],
                                                start=False, stop=(blk < half * HALF))
                        if blk >= half * HALF:
                            last = nc.tensor.matmul(ps[:, unit_bank1(half, blk), c0:c0 + P], ident_h[:], mask_kq[:],
                                                    start=False, stop=True)
                        last.then_inc(st_psum1, 1)

                pe.wait_ge(v1_ready, (b + 1) * T)
                for i in range(NP):
                    project(b * NH1, 0, i)
                for t in range(T):
                    if t % HALF == 0:
                        pe.wait_ge(qk_ready, NP + b * NH1 * NP + (2 if t == 0 else NP))
                    scores1(b * NH1, 0, t, t > 0)
                    if t < NP:
                        project(b * NH1 + 1, 1, t)
                    if t == HALF - 1:
                        turn_maxima1(b * NH1, 0, first=True)
                    if t >= HALF:
                        turned_scores1(b * NH1, 0, UNITS[0][t - HALF:t - HALF + 1], first=True)

                def head1(H, h, p, left):
                    for t in range(T):
                        n = H * T + t
                        half = t // HALF
                        pe.wait_ge(att1_ready, PLACES + n - 1)
                        for blk in range(t + 1):
                            if t % HALF == 0:
                                pe.wait_ge(e_ready1, H * NU + unit_index(half, blk) + 1)
                            if t % HALF != 0 and blk == t:
                                pe.wait_ge(e_ready1, H * NU + unit_index(half, blk) + 1)
                            last = nc.tensor.matmul(ps[:, 4 + t % 2, 0:D + 1],
                                                    big1[:, half, blk, bass.ds(t % HALF * P, P)],
                                                    v1[:, bass.ds(h, 1), blk, :].rearrange("p a c -> p (a c)"),
                                                    start=(blk == 0), stop=(blk == t))
                        last.then_inc(pv1_psum, 1)
                        if t == 0:
                            if left >= 2:
                                project(H + 2, p, 0)
                            turn_maxima1(H, 1)
                        if left >= 1:
                            if t == HALF:
                                turn_maxima1(H + 1, 0)
                            if t % HALF == 0:
                                pe.wait_ge(qk_ready, NP + (H + 1) * NP + (2 if t == 0 else NP))
                            pe.wait_ge(s1_max, (H + 1) * T + t)
                            scores1(H + 1, 1 - p, t, False)
                        if t < HALF:
                            turned_scores1(H, p, [UNITS[1][i] for i in LATE[t]])
                        elif left >= 1:
                            turned_scores1(H + 1, 1 - p, [UNITS[0][i] for i in EARLY1[t - HALF]])
                        if t > 0 and t in PART_TILES and left >= 2:
                            project(H + 2, p, PART_TILES.index(t))

                each_head1(pe, b, head1)

                def turn_output1(t):
                    if t == 0:
                        pe.wait_ge(att1_ready, PLACES + (b + 1) * NH1 * T)
                    if t >= 2:
                        pe.wait_ge(at1_ready, b * T + t - 1)
                    for f in range(4):
                        last = nc.tensor.transpose(ps[:, t % 2, f * P:(f + 1) * P], att1[:, t, f * P:(f + 1) * P], ident[:])
                    last.then_inc(at1_psum, 1)

                turn_output1(0)
                for t in range(T):
                    if t + 1 < T:
                        turn_output1(t + 1)
                    if t >= 2:
                        pe.wait_ge(prod1_ready, b * T + t - 1)
                    pe.wait_ge(at1_ready, b * T + t + 1)
                    for f in range(4):
                        last = nc.tensor.matmul(ps[:, 4 + t % 2, 0:C], att_t[t % 2][:, f, :],
                                                wt[:, col["o1"] + f * P:col["o1"] + (f + 1) * P],
                                                start=(f == 0), stop=(f == 3))
                    last.then_inc(y1_psum, 1)


_INS = ['L0_attn_hidden_states', 'L0_attn_w_q', 'L0_attn_w_k', 'L0_attn_w_v', 'L0_attn_w_o', 'L0_attn_w_kgen',
        'L0_attn_b_kgen', 'L0_attn_w_conv', 'L0_attn_b_conv', 'L0_ffn_Wr', 'L0_ffn_br', 'L0_ffn_W1', 'L0_ffn_b1',
        'L0_ffn_W2', 'L0_ffn_b2', 'L1_attn_Wqkv', 'L1_attn_Wo', 'L1_ffn_router_w', 'L1_ffn_router_b', 'L1_ffn_w1',
        'L1_ffn_b1', 'L1_ffn_w2', 'L1_ffn_b2']


def position_table(seq, dim):
    pos = np.arange(seq, dtype=np.float32)[:, None]
    div = np.exp(np.arange(0, dim, 2, dtype=np.float32) * np.float32(-np.log(10000.0) / dim))
    ang = pos * div
    return np.ascontiguousarray(np.stack([np.sin(ang), np.cos(ang)], axis=-1).reshape(seq, dim).T.astype(np.float32))


def kernel(**inputs):
    import concourse.bacc as _bacc
    from concourse.bass_utils import run_bass_kernel_spmd as _run

    nc = _bacc.Bacc("TRN2", target_bir_lowering=False, num_devices=1)
    arrays = {f"in_{name}": np.ascontiguousarray(inputs[name]) for name in _INS}
    seq = inputs['L0_attn_hidden_states'].shape[1]
    arrays["in_positions"] = position_table(seq, 64)
    args = [nc.dram_tensor(n, a.shape, mybir.dt.from_np(a.dtype), kind="ExternalInput").ap()
            for n, a in arrays.items()]
    shape = inputs['L0_attn_hidden_states'].shape
    args.append(nc.dram_tensor("out_x", shape, F32, kind="ExternalOutput").ap())
    gated_layers(nc, *args)
    r = _run(nc, [arrays], core_ids=[0])
    return r.results[0]["out_x"]
```
